# Optimizing a Trainium2 kernel written in Bass

```python
import numpy as np
import jax
import jax.numpy as jnp

def _softmax(x, axis=-1):
    return jax.nn.softmax(x, axis=axis)

def _gelu(x):
    return jax.nn.gelu(x, approximate=True)

def _silu(x):
    return jax.nn.silu(x)

def _sigmoid(x):
    return jax.nn.sigmoid(x)

def _layernorm(x, axis=-1, eps=1e-05):
    m = jnp.mean(x, axis=axis, keepdims=True)
    v = jnp.var(x, axis=axis, keepdims=True)
    return (x - m) / jnp.sqrt(v + eps)

def _scatter_add(tgt, idx, src, axis=0):
    return tgt.at[idx].add(src)

def _segment_sum(src, seg, n):
    return jax.ops.segment_sum(src, seg, n)
kernel_name = 'mk_adj_preln_d1_adj_r2_3ef6f4'

def setup_inputs(seed: int=0):
    np.random.seed(seed)
    _w = jnp.asarray

    def _rec_inputs():
        import jax
        import jax.numpy as jnp
        _gk = jax.random.key(seed)
        x = -0.0002928 + 1 * jax.random.normal(jax.random.fold_in(_gk, 1), (2048, 512), jnp.float32)
        _a = jax.random.bernoulli(jax.random.fold_in(_gk, 2), 0.000976562, (2048, 2048))
        _a = jnp.logical_or(_a, jnp.eye(2048, dtype=bool))
        _af = _a.astype(jnp.float32)
        _af = _af * jax.random.uniform(jax.random.fold_in(_gk, 3), (2048, 2048), jnp.float32, 0.05, 1)
        adj = _af
        return (x, adj)
    x, adj = _rec_inputs()

    def _L0_gnn_setup():
        import jax, jax.numpy as jnp
        import numpy as np
        D_IN, D_ATTN, STEPS = (512, 64, 2)
        P_TOP, TAU, LN_EPS = (0.9, 1.0, 1e-05)
        N = 2048

        def _xavier(key, shape):
            fan_in, fan_out = (shape[0], shape[1])
            lim = jnp.sqrt(6.0 / (fan_in + fan_out))
            return jax.random.uniform(key, shape, jnp.float32, -lim, lim)

        def _adj_from_feats(Xa, W1, W2, W3):
            Q = Xa @ W1
            K = Xa @ W3
            logits = Q @ W2 @ K.T / TAU
            n = logits.shape[1]
            order = jnp.argsort(-logits, axis=1)
            vals = jnp.take_along_axis(logits, order, axis=1)
            probs = jax.nn.softmax(vals, axis=1)
            csum = jnp.cumsum(probs, axis=1)
            k_i = jnp.sum(csum < P_TOP, axis=1) + 1
            keep = jnp.arange(n)[None, :] < k_i[:, None]
            masked_sorted = jnp.where(keep, vals, -jnp.inf)
            rows = jnp.arange(n)[:, None]
            masked = jnp.full_like(logits, -jnp.inf).at[rows, order].set(masked_sorted)
            return jax.nn.softmax(masked, axis=1)
        key = jax.random.key(seed)
        ks = jax.random.split(key, 12)
        X = jax.random.normal(ks[0], (N, D_IN), jnp.float32)
        S = jax.random.uniform(ks[1], (N, N), jnp.float32)
        W1 = _xavier(ks[2], (D_IN, D_ATTN))
        W3 = _xavier(ks[3], (D_IN, D_ATTN))
        W2 = _xavier(ks[4], (D_ATTN, D_ATTN))
        U1_0 = _xavier(ks[5], (D_IN, D_IN))
        U1_1 = _xavier(ks[6], (D_IN, D_IN))
        U2_0 = _xavier(ks[7], (D_IN, D_IN))
        U2_1 = _xavier(ks[8], (D_IN, D_IN))
        gamma = jnp.ones((D_IN,), jnp.float32)
        beta = jnp.zeros((D_IN,), jnp.float32)
        return {'X': X, 'S': S, 'W1': W1, 'W2': W2, 'W3': W3, 'U1_0': U1_0, 'U1_1': U1_1, 'U2_0': U2_0, 'U2_1': U2_1, 'gamma': gamma, 'beta': beta}
    _L0_gnn_all = _L0_gnn_setup()
    _L0_gnn_in = {k: v for k, v in _L0_gnn_all.items() if k in ('W1', 'W2', 'W3', 'U1_0', 'U1_1', 'U2_0', 'U2_1', 'gamma', 'beta')}
    del _L0_gnn_all
    return {'x': x, 'adj': adj, 'L0_gnn_W1': _L0_gnn_in['W1'], 'L0_gnn_W2': _L0_gnn_in['W2'], 'L0_gnn_W3': _L0_gnn_in['W3'], 'L0_gnn_U1_0': _L0_gnn_in['U1_0'], 'L0_gnn_U1_1': _L0_gnn_in['U1_1'], 'L0_gnn_U2_0': _L0_gnn_in['U2_0'], 'L0_gnn_U2_1': _L0_gnn_in['U2_1'], 'L0_gnn_gamma': _L0_gnn_in['gamma'], 'L0_gnn_beta': _L0_gnn_in['beta']}

def reference(x, adj, L0_gnn_W1, L0_gnn_W2, L0_gnn_W3, L0_gnn_U1_0, L0_gnn_U1_1, L0_gnn_U2_0, L0_gnn_U2_1, L0_gnn_gamma, L0_gnn_beta):
    import jax
    import jax.numpy as jnp

    def _L0_gnn_ref(X, S, W1, W2, W3, U1_0, U1_1, U2_0, U2_1, gamma, beta):
        import jax, jax.numpy as jnp
        import numpy as np
        D_IN, D_ATTN, STEPS = (512, 64, 2)
        P_TOP, TAU, LN_EPS = (0.9, 1.0, 1e-05)
        N = 2048

        def _xavier(key, shape):
            fan_in, fan_out = (shape[0], shape[1])
            lim = jnp.sqrt(6.0 / (fan_in + fan_out))
            return jax.random.uniform(key, shape, jnp.float32, -lim, lim)

        def _adj_from_feats(Xa, W1, W2, W3):
            Q = Xa @ W1
            K = Xa @ W3
            logits = Q @ W2 @ K.T / TAU
            n = logits.shape[1]
            order = jnp.argsort(-logits, axis=1)
            vals = jnp.take_along_axis(logits, order, axis=1)
            probs = jax.nn.softmax(vals, axis=1)
            csum = jnp.cumsum(probs, axis=1)
            k_i = jnp.sum(csum < P_TOP, axis=1) + 1
            keep = jnp.arange(n)[None, :] < k_i[:, None]
            masked_sorted = jnp.where(keep, vals, -jnp.inf)
            rows = jnp.arange(n)[:, None]
            masked = jnp.full_like(logits, -jnp.inf).at[rows, order].set(masked_sorted)
            return jax.nn.softmax(masked, axis=1)
        n = X.shape[0]
        S = S + jnp.eye(n, dtype=X.dtype)
        R = S / jnp.clip(S.sum(axis=1, keepdims=True), 1e-12)
        Z = jnp.zeros_like(X)
        Xf, Xa = (X, X)
        U1s, U2s = ((U1_0, U1_1), (U2_0, U2_1))
        for s in range(STEPS):
            A = _adj_from_feats(Xa, W1, W2, W3)
            Xf = R @ Xf
            Xa = A @ Xa
            Z = Z + (Xf @ U1s[s] + Xa @ U2s[s])
        Y = X + Z
        mu = Y.mean(axis=-1, keepdims=True)
        var = Y.var(axis=-1, keepdims=True)
        return (Y - mu) * jax.lax.rsqrt(var + LN_EPS) * gamma + beta
    h = jnp.maximum(_layernorm(x, axis=-1), 0.0)
    x = x + _L0_gnn_ref(h, adj, L0_gnn_W1, L0_gnn_W2, L0_gnn_W3, L0_gnn_U1_0, L0_gnn_U1_1, L0_gnn_U2_0, L0_gnn_U2_1, L0_gnn_gamma, L0_gnn_beta)
    return x

_drawn_inputs = setup_inputs


def setup_inputs(seed=0):
    import zlib

    import numpy as np

    out = dict(_drawn_inputs(seed))
    spreads = {'L0_gnn_gamma': (1.0, 0.2), 'L0_gnn_beta': (0.0, 0.1)}
    factors = {}
    for name, (base, spread) in spreads.items():
        noise = np.random.default_rng([zlib.crc32(name.encode()), seed]).standard_normal(out[name].shape)
        drawn = base * np.exp(spread * noise) if base else spread * noise
        out[name] = jnp.asarray(drawn.astype(out[name].dtype))
    for name, factor in factors.items():
        out[name] = (out[name] * factor).astype(out[name].dtype)
    return out
```

```python
import concourse.bass as bass
from concourse import mybir
from contextlib import ExitStack

F32 = mybir.dt.float32
F16 = mybir.dt.float16
I32 = mybir.dt.int32
U8 = mybir.dt.uint8
ALU = mybir.AluOpType
ACT = mybir.ActivationFunctionType
AX = mybir.AxisListType.X

P = 128
TOP_P = 0.9
LN_EPS = 1e-5

SX = 64.0
SW = 64.0
SE = 1024.0
SQ = 32.0

HALVINGS = (8, 11)
ROUND = 12582912.0
SLACK = 1e-5


def bracket_steps(n_cols, halvings):
    span = (n_cols / (1.0 - TOP_P)) * 1.05
    ratio = [span ** (0.5 ** (k + 1)) for k in range(halvings)]
    steps = [(ratio[k + 1] - ratio[k + 1] / ratio[k], ratio[k + 1] / ratio[k]) for k in range(halvings - 1)]
    up = 1.0 + 2.0 ** -17
    return ratio[0], steps + [((ratio[-1] - 1.0) * up, up)]


class Chain:

    def __init__(self, eng, sem):
        self.eng, self.sem, self.n = eng, sem, 0

    def step(self, ins):
        ins.then_inc(self.sem, 1)
        self.n += 1

    def join(self):
        self.eng.wait_ge(self.sem, self.n)

    def restart(self):
        if self.n:
            self.join()
            self.eng.sem_clear(self.sem)
            self.n = 0


def gnn_layer(nc, x, adj_t, w1_t, w2, w3, u1_0, u1_1, u2_0, u2_1, gamma, beta, out):
    N, D = x.shape
    DA = w2.shape[0]
    NT, DT = N // P, D // P
    CH = 512
    NC = N // CH
    NPAIR = NT // 2
    BLK = CH // P
    lower_end = (1.0 - TOP_P) / N * (1.0 - 2.0 ** -12)

    ctx = ExitStack()
    with ctx:
        def sb(name, shape, dt=F32):
            return ctx.enter_context(nc.sbuf_tensor(name, shape, dt))

        def ps(name, shape, dt=F32):
            return ctx.enter_context(nc.psum_tensor(name, shape, dt))

        def sem(name):
            return ctx.enter_context(nc.semaphore(name))

        def split(name, shape):
            return sb(name + "_hi", shape, F16), sb(name + "_lo", shape, F16)

        h_dram = nc.dram_tensor("h_scratch", [NT, P, D], F32, kind="Internal")
        base_dram = [nc.dram_tensor(f"base_scratch{p}", [NT, P, D], F32, kind="Internal") for p in range(2)]
        v_dram = nc.dram_tensor("v_scratch", [NT, P, D], F32, kind="Internal")

        mov_hi, mov_lo = split("mov", [P, NT, D])
        feat_hi, feat_lo = split("feat_t", [P, DT, N])
        vec_hi, vec_lo = split("vec", [P, NT, D])
        e = sb("e", [P, 4, N])
        kept = sb("kept", [P, 2, N])
        scrap = sb("scrap", [P, 3, N], U8)
        at_hi, at_lo = split("a_t", [P, NT, P])
        s_in = sb("s_in", [P, N])
        s_hi, s_lo = split("s", [P, 2, N])
        query = sb("query", [P, N], F16)
        key_hi, key_lo = split("key", [P, N])
        row_in = sb("row_in", [P, 2, D])
        y_row = sb("y_row", [P, 2, D])
        ident = sb("ident", [P, P])
        ident_h = sb("ident_h", [P, P], F16)
        ones_h = sb("ones_h", [P, 1], F16)
        small = sb("small", [P, 160])
        taken = [0]

        def columns(n):
            taken[0] += n
            return small[:, taken[0] - n:taken[0]]

        stats = sb("stats", [P, 2, 6])
        mean_var = sb("mean_var", [P, 2, 2])
        rstd = columns(2)
        shift = columns(2)
        half_col = columns(1)
        goal_col = columns(1)
        minus_col = columns(1)
        row_max = columns(4)
        neg_max = columns(4)
        total = columns(4)
        s_rcp = columns(NT)
        a_rcp = columns(4)
        goal = columns(2)
        thr = columns(2)
        above = columns(2)
        hit = columns(2)
        under = columns(2)
        top8 = sb("top8", [P, 2, 8])
        cum8 = sb("cum8", [P, 2, 8])
        reached8 = sb("reached8", [P, 2, 8])
        edge = columns(2)
        sum_ge = columns(2)
        sum_gt = columns(2)
        rcp_edge = columns(2)
        n_tied = columns(2)
        n_kept = columns(2)
        cut = columns(2)
        kept_sum = columns(2)
        rcp_tied = columns(2)
        ones8 = columns(8)
        n_col = columns(1)
        neg_thr = columns(1)
        next_thr = columns(1)
        excess = columns(1)
        signs = columns(1)
        reach = columns(1)
        hold = columns(2)
        code32 = columns(32)
        code_t = columns(32)
        code_i = sb("code_i", [P, 1], I32)

        ua = [s[:, 0, :].rearrange("p (t n) -> p t n", t=DT) for s in (s_hi, s_lo)]
        ub = [s[:, 1, :].rearrange("p (t n) -> p t n", t=DT) for s in (s_hi, s_lo)]
        u_raw = [e[:, k, :].rearrange("p (t n) -> p t n", t=DT) for k in range(2)]
        qk_w = sb("qk_w", [P, 2, 2, DT, P], F16)
        w_hi, w_lo = qk_w[:, 0], qk_w[:, 1]
        last_rows = qk_w[:, :].rearrange("p a b c d -> p (a b c d)").bitcast(F32)
        gamma_b, beta_b = last_rows[:, 0:D], last_rows[:, D:2 * D]
        wk_raw = e[:, 2, 0:DT * P].rearrange("p (t n) -> p t n", t=DT)
        w1_raw = e[0:DA, 2, DT * P:DT * P + D]
        w2_raw = e[0:DA, 2, DT * P + D:DT * P + D + P]

        r_rows = [f[:, :, :].rearrange("p d n -> p (d n)").bitcast(F32).rearrange("p (q n) -> p q n", n=D)
                  for f in (feat_hi, feat_lo)]

        logits = ps("logits", [P, N])
        turn = ps("turn", [P, 2, CH])
        acc_a = ps("acc_a", [P, CH])
        acc_r = ps("acc_r", [P, CH])

        def split_hi(dst, src, scale):
            return nc.scalar.activation(dst, src, ACT.Copy, scale=scale)

        def split_lo(dst, src, hi, scale):
            return nc.vector.scalar_tensor_tensor(out=dst, in0=src, scalar=scale, in1=hi,
                                                  op0=ALU.mult, op1=ALU.subtract)

        def product3(psum, left, right, count, opens=True):
            for k in range(count):
                l_hi, l_lo, r_hi, r_lo = left(0, k), left(1, k), right(0, k), right(1, k)
                nc.tensor.matmul(psum, l_hi, r_hi, start=(opens and k == 0), stop=False)
                nc.tensor.matmul(psum, l_hi, r_lo, start=False, stop=False)
                last = nc.tensor.matmul(psum, l_lo, r_hi, start=False,
                                        stop=(k == count - 1))
            return last

        def cols(t):
            return bass.ds(t * P, P)

        def plane(tile3, t):
            return tile3[:, bass.ds(t, 1), :].rearrange("p a d -> p (a d)")

        def dram_rows(tensor, t):
            return tensor[bass.ds(t, 1), :, :].rearrange("a p d -> p (a d)")

        def after(eng, semaphore, value):
            if not isinstance(value, int) or value > 0:
                eng.wait_ge(semaphore, value)

        def by_pairs(eng, body):
            body(0)
            with eng.Fori(1, NPAIR) as q:
                body(q)

        def stage_norm():
            const_ready = sem("const_ready")
            gp_step = sem("gp_step")
            w_loaded = sem("w_loaded")
            x_loaded = [sem(f"x_loaded{k}") for k in range(2)]
            var_ready = sem("var_ready")
            rstd_ready = sem("rstd_ready")
            shift_ready = sem("shift_ready")
            h_ready = sem("h_ready")
            h_hi_ready = sem("h_hi_ready")
            h_lo_ready = sem("h_lo_ready")
            h_turned = sem("h_turned")
            ft_hi_ready = sem("ft_hi_ready")
            ft_lo_ready = sem("ft_lo_ready")
            h_stored = [sem(f"h_stored{k}") for k in range(2)]
            w12_ready = sem("w12_ready")
            w_hi_ready = sem("w_hi_ready")
            dve_step = sem("norm_dve_step")

            with nc.Block() as block:
                @block.sync
                def _(sp):
                    w3_rows = w3.rearrange("(t p) n -> p t n", p=P)
                    sp.dma_start(w1_raw, w1_t).then_inc(w_loaded, 16)
                    sp.dma_start(w2_raw[:, 0:DA], w2).then_inc(w_loaded, 16)
                    sp.dma_start(w2_raw[:, DA:P], w2).then_inc(w_loaded, 16)
                    sp.dma_start(wk_raw[:, :, 0:DA], w3_rows).then_inc(w_loaded, 16)
                    sp.dma_start(wk_raw[:, :, DA:P], w3_rows).then_inc(w_loaded, 16)

                    def pair(q):
                        for k in range(2):
                            t = q * 2 + k
                            after(sp, h_ready, t - 1)
                            sp.dma_start(row_in[:, k, :], x[cols(t), :]).then_inc(x_loaded[k], 16)
                        for k in range(2):
                            t = q * 2 + k
                            sp.wait_ge(h_ready, t + 1)
                            sp.dma_start(dram_rows(h_dram, t), y_row[:, k, :]).then_inc(h_stored[k], 16)
                    by_pairs(sp, pair)
                    sp.wait_ge(w_loaded, 16 * 5)
                    for k in range(2):
                        sp.wait_ge(h_stored[k], 16 * NPAIR)

                @block.gpsimd
                def _(gp):
                    nc.gpsimd.memset(ident[:, :], 0.0).then_inc(gp_step, 1)
                    nc.gpsimd.memset(half_col[:, :], -0.5).then_inc(gp_step, 1)
                    gp.wait_ge(gp_step, 2)
                    nc.gpsimd.affine_select(out=ident[:, :], in_=ident[:, :], compare_op=ALU.not_equal, fill=1.0,
                                            base=0, pattern=[[-1, P]], channel_multiplier=1).then_inc(gp_step, 1)
                    gp.wait_ge(gp_step, 3)
                    nc.gpsimd.tensor_copy(ident_h[:, :], ident[:, :]).then_inc(const_ready, 1)
                    nc.gpsimd.memset(ones_h[:, :], 1.0)
                    nc.gpsimd.memset(ones8[:, :], 1.0)
                    nc.gpsimd.memset(minus_col[:, :], -1.0)
                    nc.gpsimd.memset(goal_col[:, :], TOP_P)
                    nc.gpsimd.memset(n_col[:, :], float(N))
                    nc.gpsimd.memset(code32[:, :], 0.0)

                    def pair(q):
                        for k in range(2):
                            t = q * 2 + k
                            gp.wait_ge(var_ready, t + 1)
                            after(gp, h_ready, t - 1)
                            nc.gpsimd.tensor_tensor(rstd[:, k:k + 1], mean_var[:, k, 1:2], half_col[:, :],
                                                    ALU.pow).then_inc(rstd_ready, 1)
                    by_pairs(gp, pair)

                @block.vector
                def _(dve):
                    ch = Chain(dve, dve_step)
                    nc.vector.memset(key_lo[:, :], 0.0)
                    dve.wait_ge(w_hi_ready, 1)
                    split_lo(w_lo[:, 0].rearrange("p t n -> p (t n)"), acc_a[:, :],
                             w_hi[:, 0].rearrange("p t n -> p (t n)"), SW)
                    dve.wait_ge(w_hi_ready, 2)
                    split_lo(w_lo[:, 1], wk_raw, w_hi[:, 1], SW)

                    def pair(q):
                        for k in range(2):
                            t = q * 2 + k
                            after(dve, rstd_ready, t - 1)
                            after(dve, shift_ready, t - 1)
                            dve.wait_ge(x_loaded[k], (q + 1) * 16)
                            ch.step(nc.vector.bn_stats(stats[:, k, :], row_in[:, k, :]))
                            ch.join()
                            ch.step(nc.vector.bn_aggr(mean_var[:, k, :], stats[:, k, :]))
                            ch.join()
                            nc.vector.tensor_scalar(mean_var[:, k, 1:2], mean_var[:, k, 1:2], LN_EPS, None,
                                                    ALU.add).then_inc(var_ready, 1)
                        for k in range(2):
                            t = q * 2 + k
                            dve.wait_ge(rstd_ready, t + 1)
                            after(dve, h_ready, t - 1)
                            nc.vector.scalar_tensor_tensor(out=shift[:, k:k + 1], in0=mean_var[:, k, 0:1], scalar=-1.0,
                                                           in1=rstd[:, k:k + 1], op0=ALU.mult,
                                                           op1=ALU.mult).then_inc(shift_ready, 1)
                        for k in range(2):
                            t = q * 2 + k
                            dve.wait_ge(h_hi_ready, t + 1)
                            split_lo(plane(mov_lo, t), y_row[:, k, :], plane(mov_hi, t), SX).then_inc(h_lo_ready, 1)
                            dve.wait_ge(ft_hi_ready, t + 1)
                            split_lo(feat_lo[:, :, cols(t)], turn[:, k, :].rearrange("p (d n) -> p d n", d=DT),
                                     feat_hi[:, :, cols(t)], SX).then_inc(ft_lo_ready, 1)
                        ch.restart()
                    by_pairs(dve, pair)

                @block.scalar
                def _(act):
                    act.wait_ge(w12_ready, 1)
                    split_hi(w_hi[:, 0].rearrange("p t n -> p (t n)"), acc_a[:, :], SW).then_inc(w_hi_ready, 1)
                    act.wait_ge(w_loaded, 16 * 5)
                    split_hi(w_hi[:, 1], wk_raw, SW).then_inc(w_hi_ready, 1)

                    def pair(q):
                        for k in range(2):
                            t = q * 2 + k
                            act.wait_ge(shift_ready, t + 1)
                            after(act, h_stored[k], q * 16)
                            after(act, h_lo_ready, t - 1)
                            after(act, h_turned, t - 1)
                            nc.scalar.activation(y_row[:, k, :], row_in[:, k, :], ACT.Relu, bias=shift[:, k:k + 1],
                                                 scale=rstd[:, k:k + 1]).then_inc(h_ready, 1)
                        for k in range(2):
                            t = q * 2 + k
                            act.wait_ge(h_ready, t + 1)
                            split_hi(plane(mov_hi, t), y_row[:, k, :], SX).then_inc(h_hi_ready, 1)
                            act.wait_ge(h_turned, t + 1)
                            split_hi(feat_hi[:, :, cols(t)], turn[:, k, :].rearrange("p (d n) -> p d n", d=DT),
                                     SX).then_inc(ft_hi_ready, 1)
                    by_pairs(act, pair)

                @block.tensor
                def _(pe):
                    pe.wait_ge(w_loaded, 16 * 5)
                    for d in range(DT):
                        last = nc.tensor.matmul(acc_a[:, d * P:(d + 1) * P], w1_raw[:, d * P:(d + 1) * P], w2_raw,
                                                start=True, stop=True)
                    last.then_inc(w12_ready, 1)
                    pe.wait_ge(const_ready, 1)

                    def pair(q):
                        for k in range(2):
                            t = q * 2 + k
                            pe.wait_ge(h_ready, t + 1)
                            after(pe, ft_lo_ready, t - 1)
                            for d in range(DT):
                                last = nc.tensor.transpose(turn[:, k, d * P:(d + 1) * P],
                                                           y_row[:, k, d * P:(d + 1) * P], ident[:, :])
                            last.then_inc(h_turned, 1)
                    by_pairs(pe, pair)

        def stage_project(p):
            w_a, w_b = ((u1_1, u1_0), (u2_1, u2_0))[p]
            dst_hi, dst_lo = ((vec_hi, vec_lo), (mov_hi, mov_lo))[p]
            u_loaded = sem(f"u_loaded{p}")
            u_hi_ready = sem(f"u_hi_ready{p}")
            u_lo_ready = sem(f"u_lo_ready{p}")
            qk_done = sem(f"qk_done{p}")
            qk_hi_ready = sem(f"qk_hi_ready{p}")
            qk_lo_ready = sem(f"qk_lo_ready{p}")
            prod_done = sem(f"prod_done{p}")
            dst_hi_ready = sem(f"dst_hi_ready{p}")
            dst_lo_ready = sem(f"dst_lo_ready{p}")
            base_ready = sem(f"base_ready{p}")
            base_stored = [sem(f"base_stored{p}_{k}") for k in range(2)]
            h_loaded = [sem(f"h_loaded{p}_{k}") for k in range(2)]
            v_loaded = [sem(f"v_loaded{p}_{k}") for k in range(2)]
            v_hi_ready = sem(f"v_hi_ready{p}")
            v_lo_ready = sem(f"v_lo_ready{p}")

            with nc.Block() as block:
                @block.sync
                def _(sp):
                    for k, w in enumerate((w_a, w_b)):
                        sp.dma_start(u_raw[k], w.rearrange("(t p) n -> p t n", p=P)).then_inc(u_loaded, 16)

                    def pair(q):
                        if p == 1:
                            for k in range(2):
                                t = q * 2 + k
                                after(sp, base_stored[k], q * 16)
                                sp.dma_start(row_in[:, k, :], dram_rows(h_dram, t)).then_inc(h_loaded[k], 16)
                                after(sp, v_lo_ready, t - 1)
                                sp.dma_start(y_row[:, k, :], dram_rows(v_dram, t)).then_inc(v_loaded[k], 16)
                        for k in range(2):
                            t = q * 2 + k
                            sp.wait_ge(base_ready, t + 1)
                            sp.dma_start(dram_rows(base_dram[p], t), row_in[:, k, :]).then_inc(base_stored[k], 16)
                    by_pairs(sp, pair)
                    for k in range(2):
                        sp.wait_ge(base_stored[k], 16 * NPAIR)

                @block.tensor
                def _(pe):
                    for c in range(NC):
                        for w in range(2):
                            after(pe, qk_lo_ready, 2 * c + w - 1)
                            product3(turn[:, w, :], lambda part, d: (w_hi, w_lo)[part][:, w, d, :],
                                     lambda part, d: (feat_hi, feat_lo)[part][:, d, c * CH:(c + 1) * CH],
                                     DT).then_inc(qk_done, 1)
                    pe.wait_ge(u_lo_ready, 2)

                    def pair(q):
                        for k in range(2):
                            t = q * 2 + k
                            for w, u in enumerate((ua, ub)):
                                after(pe, (dst_lo_ready, base_ready)[w], t - 1)
                                bank = 2 * w + k
                                product3(logits[:, bank * CH:(bank + 1) * CH],
                                         lambda part, d: (feat_hi, feat_lo)[part][:, d, cols(t)],
                                         lambda part, d: u[part][:, d, :], DT).then_inc(prod_done, 1)
                    by_pairs(pe, pair)

                @block.scalar
                def _(act):
                    act.wait_ge(u_loaded, 32)
                    for k, u in enumerate((ua, ub)):
                        split_hi(u[0], u_raw[k], SW).then_inc(u_hi_ready, 1)
                    for c in range(NC):
                        for w in range(2):
                            act.wait_ge(qk_done, 2 * c + w + 1)
                            split_hi((query, key_hi)[w][:, c * CH:(c + 1) * CH], turn[:, w, :],
                                     SQ / (SX * SW)).then_inc(qk_hi_ready, 1)

                    def pair(q):
                        for k in range(2):
                            t = q * 2 + k
                            act.wait_ge(prod_done, t * 2 + 1)
                            split_hi(plane(dst_hi, t), logits[:, k * CH:(k + 1) * CH],
                                     1.0 / SW).then_inc(dst_hi_ready, 1)
                            if p == 1:
                                act.wait_ge(v_loaded[k], (q + 1) * 16)
                                split_hi(plane(vec_hi, t), y_row[:, k, :], SX).then_inc(v_hi_ready, 1)
                    by_pairs(act, pair)

                @block.vector
                def _(dve):
                    for k, u in enumerate((ua, ub)):
                        dve.wait_ge(u_hi_ready, k + 1)
                        split_lo(u[1], u_raw[k], u[0], SW).then_inc(u_lo_ready, 1)
                    for c in range(NC):
                        for w in range(2):
                            dve.wait_ge(qk_hi_ready, 2 * c + w + 1)
                            lo, hi = ((DA, P), (0, DA))[w]
                            span = slice(c * CH, (c + 1) * CH)
                            split_lo((query, key_lo)[w][lo:hi, span], turn[lo:hi, w, :],
                                     (query, key_hi)[w][lo:hi, span], SQ / (SX * SW)).then_inc(qk_lo_ready, 1)

                    def pair(q):
                        for k in range(2):
                            t = q * 2 + k
                            dve.wait_ge(dst_hi_ready, t + 1)
                            split_lo(plane(dst_lo, t), logits[:, k * CH:(k + 1) * CH], plane(dst_hi, t),
                                     1.0 / SW).then_inc(dst_lo_ready, 1)
                            dve.wait_ge(prod_done, t * 2 + 2)
                            after(dve, base_stored[k], q * 16)
                            bank = logits[:, (2 + k) * CH:(3 + k) * CH]
                            if p == 0:
                                nc.vector.tensor_scalar(row_in[:, k, :], bank, 1.0 / (SX * SW), None,
                                                        ALU.mult).then_inc(base_ready, 1)
                            else:
                                dve.wait_ge(h_loaded[k], (q + 1) * 16)
                                nc.vector.scalar_tensor_tensor(
                                    out=row_in[:, k, :], in0=bank, scalar=1.0 / (SX * SW), in1=row_in[:, k, :],
                                    op0=ALU.mult, op1=ALU.add).then_inc(base_ready, 1)
                                dve.wait_ge(v_hi_ready, t + 1)
                                split_lo(plane(vec_lo, t), y_row[:, k, :], plane(vec_hi, t),
                                         SX).then_inc(v_lo_ready, 1)
                    by_pairs(dve, pair)

        def stage_multiply(p):
            final = p == 1
            halvings = HALVINGS[p]
            first_ratio, steps = bracket_steps(N, halvings)
            s_loaded = sem(f"s_loaded{p}")
            s_hi_ready = sem(f"s_hi_ready{p}")
            s_lo_ready = sem(f"s_lo_ready{p}")
            base_loaded = [sem(f"base_loaded{p}_{k}") for k in range(2)]
            logits_done = sem(f"logits_done{p}")
            max_ready = sem(f"max_ready{p}")
            exp_ready = sem(f"exp_ready{p}")
            kept_ready = sem(f"kept_ready{p}")
            a_turned = sem(f"a_turned{p}")
            at_hi_ready = sem(f"at_hi_ready{p}")
            at_lo_ready = sem(f"at_lo_ready{p}")
            s_sum_done = sem(f"s_sum_done{p}")
            s_rcp_ready = sem(f"s_rcp_ready{p}")
            r_done = sem(f"r_done{p}")
            r_read = sem(f"r_read{p}")
            a_done = sem(f"a_done{p}")
            y_ready = sem(f"y_ready{p}")
            search_step = sem(f"search_step{p}")
            thr_set = sem(f"thr_set{p}")
            sums_ready = sem(f"sums_ready{p}")
            thr_final = sem(f"thr_final{p}")
            update_step = sem(f"update_step{p}")
            if final:
                last_loaded = sem("last_loaded")
                x_loaded = [sem(f"last_x_loaded{k}") for k in range(2)]
                var_ready = sem("last_var_ready")
                rstd_ready = sem("last_rstd_ready")
                normed = sem("normed")
                out_stored = [sem(f"out_stored{k}") for k in range(2)]
            else:
                y_turned = sem("y_turned")
                y_hi_ready = sem("y_hi_ready")
                y_lo_ready = sem("y_lo_ready")
                v_stored = [sem(f"v_stored{k}") for k in range(2)]

            ACT_AT, DVE_AT = (((2, 3, 5, 6, 7), (0, 3, 6)), ((2, 3, 5, 7, 8), (0, 4, 8)))[p]

            FINISH_AT = {0: ((0, 0),), 1: ((1, 0),), 3: ((0, 1),), 4: ((0, 2),), 5: ((0, 3),),
                         6: ((1, 1),), 7: ((1, 2),), 8: ((1, 3),)}

            def skewed(eng, body):
                body(0, 0, False, False, True, True)
                body(1, 1, False, True, True, True)
                with eng.Fori(1, NPAIR // 2 - 1) as i:
                    body(i * 2, 0, True, True, True, True)
                    body(i * 2 + 1, 1, True, True, True, True)
                body(NPAIR - 2, 0, True, True, True, True)
                body(NPAIR - 1, 1, True, True, True, False)
                body(NPAIR, 0, True, True, False, False)
                if final:
                    body(NPAIR + 1, 1, True, False, False, False)

            with nc.Block() as block:
                @block.sync
                def _(sp):
                    def load_s(t):
                        after(sp, s_lo_ready, t)
                        sp.dma_start(s_in[:, :], adj_t[bass.ds(t, 1), :, :].rearrange("a p n -> p (a n)")
                                     ).then_inc(s_loaded, 16)

                    def load_base(t, k):
                        sp.dma_start(row_in[:, k, :], dram_rows(base_dram[p], t)).then_inc(base_loaded[k], 16)

                    load_s(0)
                    for k in range(2):
                        load_base(k, k)
                    if final:
                        for dst, row in ((gamma_b, gamma), (beta_b, beta)):
                            sp.dma_start(dst, row.rearrange("(a d) -> a d", a=1).to_broadcast([P, D])
                                         ).then_inc(last_loaded, 16)

                    def pair(q, half, before_last, last, this, after_this):
                        if this:
                            load_s(q * 2 + 1)
                        for k in range(2):
                            if k and after_this:
                                load_s(q * 2 + 2)
                            if this:
                                sp.wait_ge(r_read, q * 2 + k + 1)
                                if not final:
                                    sp.dma_start(dram_rows(v_dram, q * 2 + k), row_in[:, k, :]
                                                 ).then_inc(v_stored[k], 16)
                                    sp.wait_ge(v_stored[k], (q + 1) * 16)
                            if after_this:
                                load_base(q * 2 + 2 + k, k)
                    skewed(sp, pair)
                    if final:
                        sp.wait_ge(last_loaded, 32)
                    else:
                        for k in range(2):
                            sp.wait_ge(v_stored[k], 16 * NPAIR)

                @block.gpsimd
                def _(gp):
                    if final:
                        gp.wait_ge(last_loaded, 32)

                    ch = Chain(gp, update_step)
                    CHUNKS = 4

                    def s_low(t, slot, c):
                        gp.wait_ge(s_hi_ready, t + 1)
                        span = slice(c * N // CHUNKS, (c + 1) * N // CHUNKS)
                        ins = nc.gpsimd.tensor_tensor(s_lo[:, slot, span], s_in[:, span], s_hi[:, slot, span],
                                                      ALU.subtract)
                        if c == CHUNKS - 1:
                            ins.then_inc(s_lo_ready, 1)

                    for c in range(CHUNKS):
                        s_low(0, 0, c)

                    def start_second(q, half):
                        tot = total[:, 2 * half + 1:2 * half + 2]
                        gp.wait_ge(exp_ready, q * 2 + 2)
                        after(gp, kept_ready, q * 2)
                        ch.step(nc.gpsimd.tensor_tensor(goal[:, 1:2], tot, goal_col[:, :], ALU.mult))
                        ch.step(nc.gpsimd.tensor_scalar(neg_thr[:, :], tot, -lower_end * first_ratio, None, ALU.mult))
                        ch.join()
                        gp.sem_inc(thr_set, 1)

                    def halve_second(q, h):
                        gain, miss = steps[h]
                        ch.step(nc.gpsimd.tensor_scalar(next_thr[:, :], neg_thr[:, :], gain, None, ALU.mult))
                        gp.wait_ge(sums_ready, q * (2 * halvings) + 2 * h + 2)
                        ch.step(nc.gpsimd.tensor_tensor(reach[:, :], signs[:, :], n_col[:, :], ALU.add))
                        ch.join()
                        ch.step(nc.gpsimd.tensor_scalar(reach[:, :], reach[:, :], -0.5, neg_thr[:, :],
                                                        ALU.mult, ALU.mult))
                        ch.join()
                        ch.step(nc.gpsimd.tensor_scalar(reach[:, :], reach[:, :], excess[:, :], goal[:, 1:2],
                                                        ALU.add, ALU.is_ge))
                        ch.join()
                        ch.step(nc.gpsimd.tensor_scalar(neg_thr[:, :], reach[:, :], miss / gain, next_thr[:, :],
                                                        ALU.add, ALU.mult))
                        ch.join()
                        if h < halvings - 1:
                            gp.sem_inc(thr_set, 1)
                        else:
                            nc.gpsimd.tensor_tensor(thr[:, 1:2], neg_thr[:, :], minus_col[:, :],
                                                    ALU.mult).then_inc(thr_final, 1)

                    def finish_row(q, k, part):
                        t = q * 2 - 4 + k
                        y, r_part = y_row[:, k, :], plane(r_rows[k], q - 2)
                        if part == 0:
                            gp.wait_ge(var_ready, t + 1)
                            ch.step(nc.gpsimd.tensor_tensor(rstd[:, k:k + 1], mean_var[:, k, 1:2], half_col[:, :],
                                                            ALU.pow))
                            ch.join()
                            gp.sem_inc(rstd_ready, 1)
                            gp.dma_start(r_part, x[cols(t), :]).then_inc(x_loaded[k], 16)
                        if part == 1:
                            gp.wait_ge(normed, t + 1)
                            ch.step(nc.gpsimd.tensor_tensor(y, y, gamma_b, ALU.mult))
                            ch.join()
                        if part == 2:
                            gp.wait_ge(x_loaded[k], (q - 1) * 16)
                            ch.step(nc.gpsimd.tensor_tensor(y, y, beta_b, ALU.add))
                            ch.join()
                        if part == 3:
                            ch.step(nc.gpsimd.tensor_tensor(y, y, r_part, ALU.add))
                            ch.join()
                            gp.dma_start(out[cols(t), :], y).then_inc(out_stored[k], 16)

                    def pair(q, half, before_last, last, this, after_this):
                        if this:
                            start_second(q, half)
                        for h in range(halvings):
                            if this:
                                halve_second(q, h)
                                if h < CHUNKS:
                                    s_low(q * 2 + 1, 1, h)
                                elif h < 2 * CHUNKS and after_this:
                                    s_low(q * 2 + 2, 0, h - CHUNKS)
                            if final and before_last:
                                for k, part in FINISH_AT.get(h, ()):
                                    finish_row(q, k, part)
                        ch.restart()
                    skewed(gp, pair)
                    if final:
                        for k in range(2):
                            gp.wait_ge(out_stored[k], 16 * NPAIR)

                @block.scalar
                def _(act):
                    def s_high(t, slot):
                        act.wait_ge(s_loaded, t * 16 + 16)
                        after(act, r_done, t - 1)
                        split_hi(s_hi[:, slot, :], s_in[:, :], 1.0).then_inc(s_hi_ready, 1)

                    def exponential(t, slot):
                        act.wait_ge(max_ready, t + 1)
                        after(act, kept_ready, t - 3)
                        nc.scalar.activation(e[:, slot, :], logits[:, :], ACT.Exp, bias=neg_max[:, slot:slot + 1],
                                             scale=1.0 / (SQ * SQ), accum_out=total[:, slot:slot + 1]
                                             ).then_inc(exp_ready, 1)

                    def evaluate(q, slot, h):
                        act.wait_ge(thr_set, q * halvings + h + 1)
                        nc.scalar.activation(scrap[:, 1, :], e[:, slot, :], ACT.Relu, bias=neg_thr[:, :],
                                             accum_out=excess[:, :]).then_inc(sums_ready, 1)
                        nc.scalar.activation(scrap[:, 2, :], e[:, slot, :], ACT.Sign, bias=neg_thr[:, :],
                                             accum_out=signs[:, :]).then_inc(sums_ready, 1)

                    def a_high(t):
                        after(act, a_done, t)
                        for c in range(BLK):
                            act.wait_ge(a_turned, t * BLK + c + 1)
                            split_hi(at_hi[:, c * BLK:(c + 1) * BLK, :],
                                     turn[:, c % 2, :].rearrange("p (b n) -> p b n", b=BLK), SE
                                     ).then_inc(at_hi_ready, 1)

                    def product_out(t, k, slot):
                        act.wait_ge(a_done, t + 1)
                        after(act, y_turned, t - 1)
                        nc.scalar.activation(y_row[:, k, :], acc_a[:, :], ACT.Copy,
                                             scale=a_rcp[:, slot:slot + 1]).then_inc(y_ready, 1)
                        act.wait_ge(y_turned, t + 1)
                        split_hi(feat_hi[:, :, cols(t)], turn[:, 0, :].rearrange("p (d n) -> p d n", d=DT),
                                 SX).then_inc(y_hi_ready, 1)

                    s_high(0, 0)
                    for k in range(2):
                        exponential(k, k)

                    def pair(q, half, before_last, last, this, after_this):
                        other = 1 - half
                        if this:
                            s_high(q * 2 + 1, 1)
                        for h in range(halvings):
                            if this:
                                evaluate(q, 2 * half + 1, h)
                            if h == ACT_AT[0] and last:
                                a_high(q * 2 - 2)
                            if h == ACT_AT[1] and after_this:
                                exponential(q * 2 + 2, 2 * other)
                                s_high(q * 2 + 2, 0)
                            if h == ACT_AT[2] and last and not final:
                                product_out(q * 2 - 2, 0, 2 * other)
                            if h == ACT_AT[3] and last:
                                a_high(q * 2 - 1)
                            if h == ACT_AT[4] and after_this:
                                exponential(q * 2 + 3, 2 * other + 1)
                        if last and not final:
                            product_out(q * 2 - 1, 1, 2 * other + 1)
                    skewed(act, pair)

                @block.tensor
                def _(pe):
                    def logits_of(t):
                        after(pe, exp_ready, t)
                        for c in range(NC):
                            span = slice(c * CH, (c + 1) * CH)
                            nc.tensor.matmul(logits[:, span], query[:, cols(t)], key_hi[:, span], start=True, stop=False)
                            done = nc.tensor.matmul(logits[:, span], query[:, cols(t)], key_lo[:, span],
                                                    start=False, stop=True)
                        done.then_inc(logits_done, 1)

                    for k in range(2):
                        logits_of(k)

                    def pair(q, half, before_last, last, this, after_this):
                        for k in range(2):
                            u = q * 2 - 2 + k
                            if after_this:
                                logits_of(q * 2 + 2 + k)
                            if this:
                                t = q * 2 + k
                                pe.wait_ge(s_lo_ready, t + 1)
                                parts = [part[:, k, :].rearrange("p (j n) -> p j n", j=NT) for part in (s_hi, s_lo)]
                                if not final:
                                    after(pe, y_ready, u) if last else None
                                    after(pe, s_rcp_ready, t)
                                    for j in range(NT):
                                        nc.tensor.matmul(acc_a[:, 0:1], parts[0][:, j, :], ones_h[:, :],
                                                         start=(j == 0), stop=False)
                                        done = nc.tensor.matmul(acc_a[:, 0:1], parts[1][:, j, :], ones_h[:, :],
                                                                start=False, stop=(j == NT - 1))
                                    done.then_inc(s_sum_done, 1)
                                after(pe, r_read, t)
                                nc.tensor.matmul(acc_r[:, :], ident_h[:, :], plane(vec_hi, t), start=True, stop=False)
                                nc.tensor.matmul(acc_r[:, :], ident_h[:, :], plane(vec_lo, t), start=False, stop=False)
                                product3(acc_r[:, :], lambda part, j: parts[part][:, j, :],
                                         lambda part, j: (vec_hi, vec_lo)[part][:, j, :], NT,
                                         opens=False).then_inc(r_done, 1)
                            if last:
                                pe.wait_ge(kept_ready, u + 1)
                                for c in range(BLK):
                                    if c >= 2:
                                        pe.wait_ge(at_lo_ready, u * BLK + c - 1)
                                    elif c == 1 or final:
                                        after(pe, at_lo_ready, u * BLK - 1 + c)
                                    else:
                                        after(pe, y_lo_ready, u)
                                    for b in range(BLK):
                                        j = c * BLK + b
                                        done = nc.tensor.transpose(turn[:, c % 2, b * P:(b + 1) * P],
                                                                   kept[:, k, j * P:(j + 1) * P], ident[:, :])
                                    done.then_inc(a_turned, 1)
                                pe.wait_ge(at_lo_ready, (u + 1) * BLK)
                                after(pe, y_ready, u)
                                if not final and this:
                                    pe.wait_ge(s_rcp_ready, q * 2 + k + 1)
                                product3(acc_a[:, :], lambda part, j: (at_hi, at_lo)[part][:, j, :],
                                         lambda part, j: (mov_hi, mov_lo)[part][:, j, :], NT).then_inc(a_done, 1)
                                if not final:
                                    pe.wait_ge(y_ready, u + 1)
                                    for d in range(DT):
                                        done = nc.tensor.transpose(turn[:, 0, d * P:(d + 1) * P],
                                                                   y_row[:, k, d * P:(d + 1) * P], ident[:, :])
                                    done.then_inc(y_turned, 1)
                    skewed(pe, pair)

                @block.vector
                def _(dve):
                    ch = Chain(dve, search_step)

                    def maximum(t, slot):
                        dve.wait_ge(logits_done, t + 1)
                        ch.step(nc.vector.reduce_max(row_max[:, slot:slot + 1], logits[:, :], AX))
                        ch.join()
                        nc.vector.tensor_scalar(neg_max[:, slot:slot + 1], row_max[:, slot:slot + 1],
                                                -1.0 / (SQ * SQ), None, ALU.mult).then_inc(max_ready, 1)

                    def a_low(t):
                        for c in range(BLK):
                            dve.wait_ge(at_hi_ready, t * BLK + c + 1)
                            split_lo(at_lo[:, c * BLK:(c + 1) * BLK, :],
                                     turn[:, c % 2, :].rearrange("p (b n) -> p b n", b=BLK),
                                     at_hi[:, c * BLK:(c + 1) * BLK, :], SE).then_inc(at_lo_ready, 1)

                    def r_out(q, k):
                        t = q * 2 + k
                        rcp = s_rcp[:, bass.ds(t, 1)]
                        if not final:
                            dve.wait_ge(s_sum_done, t + 1)
                            ch.step(nc.vector.tensor_scalar(rcp, acc_a[:, 0:1], 1.0, 1e-12, ALU.add, ALU.max))
                            ch.join()
                            ch.step(nc.vector.reciprocal(rcp, rcp))
                            ch.join()
                            ch.step(nc.vector.tensor_scalar(rcp, rcp, 1.0 / SX, None, ALU.mult))
                            ch.join()
                            dve.sem_inc(s_rcp_ready, 1)
                        dve.wait_ge(r_done, t + 1)
                        dve.wait_ge(base_loaded[k], (q + 1) * 16)
                        dst = plane(r_rows[k], q) if final else row_in[:, k, :]
                        nc.vector.scalar_tensor_tensor(out=dst, in0=acc_r[:, :], scalar=rcp, in1=row_in[:, k, :],
                                                       op0=ALU.mult, op1=ALU.add).then_inc(r_read, 1)

                    def y_out(q, k, slot):
                        t = q * 2 - 2 + k
                        if not final:
                            dve.wait_ge(y_hi_ready, t + 1)
                            split_lo(feat_lo[:, :, cols(t)], turn[:, 0, :].rearrange("p (d n) -> p d n", d=DT),
                                     feat_hi[:, :, cols(t)], SX).then_inc(y_lo_ready, 1)
                            return
                        dve.wait_ge(a_done, t + 1)
                        dve.wait_ge(r_read, t + 1)
                        after(dve, out_stored[k], (q - 1) * 16)
                        nc.vector.scalar_tensor_tensor(out=y_row[:, k, :], in0=acc_a[:, :],
                                                       scalar=a_rcp[:, slot:slot + 1], in1=plane(r_rows[k], q - 1),
                                                       op0=ALU.mult, op1=ALU.add).then_inc(y_ready, 1)
                        dve.wait_ge(y_ready, t + 1)
                        ch.step(nc.vector.bn_stats(stats[:, k, :], y_row[:, k, :]))
                        ch.join()
                        ch.step(nc.vector.bn_aggr(mean_var[:, k, :], stats[:, k, :]))
                        ch.join()
                        nc.vector.tensor_scalar(mean_var[:, k, 1:2], mean_var[:, k, 1:2], LN_EPS, None,
                                                ALU.add).then_inc(var_ready, 1)

                    def normalise(q, k):
                        dve.wait_ge(rstd_ready, q * 2 - 3 + k)
                        nc.vector.tensor_scalar(y_row[:, k, :], y_row[:, k, :], mean_var[:, k, 0:1], rstd[:, k:k + 1],
                                                ALU.subtract, ALU.mult).then_inc(normed, 1)

                    def halve(slot, h):
                        gain, miss = steps[h]
                        ch.step(nc.vector.scalar_tensor_tensor(
                            out=scrap[:, 0, :], in0=e[:, slot, :], scalar=thr[:, 0:1], in1=e[:, slot, :],
                            op0=ALU.is_gt, op1=ALU.mult, accum_out=above[:, 0:1]))
                        ch.join()
                        ch.step(nc.vector.tensor_scalar(hit[:, 0:1], above[:, 0:1], goal[:, 0:1], gain,
                                                        ALU.is_ge, ALU.mult))
                        ch.join()
                        ch.step(nc.vector.tensor_scalar(thr[:, 0:1], hit[:, 0:1], miss, thr[:, 0:1],
                                                        ALU.add, ALU.mult))
                        ch.join()

                    def locate(half, tiles):
                        for k in tiles:
                            slot = 2 * half + k
                            ch.step(nc.vector.scalar_tensor_tensor(
                                out=kept[:, k, :], in0=e[:, slot, :], scalar=thr[:, k:k + 1], in1=e[:, slot, :],
                                op0=ALU.is_lt, op1=ALU.mult, accum_out=under[:, k:k + 1]))
                            ch.join()
                            ch.step(nc.vector.max(top8[:, k, :], kept[:, k, :]))
                            ch.step(nc.vector.tensor_tensor(above[:, k:k + 1], total[:, slot:slot + 1],
                                                            under[:, k:k + 1], ALU.subtract))
                            ch.join()
                            ch.step(nc.vector.tensor_tensor_scan(cum8[:, k, :], ones8[:, :], top8[:, k, :],
                                                                 above[:, k:k + 1], ALU.mult, ALU.add))
                            ch.join()
                            ch.step(nc.vector.scalar_tensor_tensor(
                                out=reached8[:, k, 0:7], in0=cum8[:, k, 0:7], scalar=goal[:, k:k + 1],
                                in1=top8[:, k, 0:7], op0=ALU.is_ge, op1=ALU.mult))
                            ch.step(nc.vector.tensor_copy(reached8[:, k, 7:8], top8[:, k, 7:8]))
                            ch.join()
                            ch.step(nc.vector.reduce_max(edge[:, k:k + 1], reached8[:, k, :], AX))
                            ch.join()
                            ch.step(nc.vector.scalar_tensor_tensor(
                                out=kept[:, k, :], in0=e[:, slot, :], scalar=edge[:, k:k + 1], in1=e[:, slot, :],
                                op0=ALU.is_ge, op1=ALU.mult, accum_out=sum_ge[:, k:k + 1]))
                            ch.step(nc.vector.scalar_tensor_tensor(
                                out=cum8[:, k, :], in0=top8[:, k, :], scalar=edge[:, k:k + 1], in1=top8[:, k, :],
                                op0=ALU.is_gt, op1=ALU.mult, accum_out=sum_gt[:, k:k + 1]))

                    def weigh(half):
                        ch.step(nc.vector.tensor_tensor(sum_gt[:, :], sum_gt[:, :], above[:, :], ALU.add))
                        ch.step(nc.vector.reciprocal(rcp_edge[:, :], edge[:, :]))
                        ch.step(nc.vector.scalar_tensor_tensor(out=hold[:, :], in0=goal[:, :], scalar=1.0 - SLACK,
                                                               in1=sum_ge[:, :], op0=ALU.mult, op1=ALU.is_gt))
                        ch.join()
                        ch.step(nc.vector.tensor_tensor(n_tied[:, :], sum_ge[:, :], sum_gt[:, :], ALU.subtract))
                        ch.step(nc.vector.tensor_tensor(n_kept[:, :], goal[:, :], sum_gt[:, :], ALU.subtract))
                        ch.join()
                        ch.step(nc.vector.tensor_tensor(n_tied[:, :], n_tied[:, :], rcp_edge[:, :], ALU.mult))
                        ch.step(nc.vector.tensor_tensor(n_kept[:, :], n_kept[:, :], rcp_edge[:, :], ALU.mult))
                        ch.join()
                        ch.step(nc.vector.tensor_scalar(n_tied[:, :], n_tied[:, :], ROUND, ROUND, ALU.add, ALU.subtract))
                        ch.step(nc.vector.tensor_scalar(n_kept[:, :], n_kept[:, :], 0.495, ROUND, ALU.add, ALU.add))
                        ch.join()
                        ch.step(nc.vector.tensor_scalar(n_tied[:, :], n_tied[:, :], 1.0, None, ALU.max))
                        ch.step(nc.vector.tensor_scalar(n_kept[:, :], n_kept[:, :], ROUND, 1.0, ALU.subtract, ALU.max))
                        ch.join()
                        ch.step(nc.vector.tensor_tensor(n_kept[:, :], n_kept[:, :], n_tied[:, :], ALU.min))
                        ch.step(nc.vector.reciprocal(rcp_tied[:, :], n_tied[:, :]))
                        ch.join()
                        ch.step(nc.vector.tensor_tensor(cut[:, :], n_tied[:, :], n_kept[:, :], ALU.subtract))
                        ch.join()
                        ch.step(nc.vector.tensor_scalar(n_kept[:, :], cut[:, :], 1.0, None, ALU.min))
                        ch.step(nc.vector.tensor_tensor(cut[:, :], cut[:, :], edge[:, :], ALU.mult))
                        ch.join()
                        ch.step(nc.vector.scalar_tensor_tensor(out=n_kept[:, :], in0=hold[:, :], scalar=16.0,
                                                               in1=n_kept[:, :], op0=ALU.mult, op1=ALU.max))
                        ch.step(nc.vector.tensor_tensor(kept_sum[:, :], sum_ge[:, :], cut[:, :], ALU.subtract))
                        ch.join()
                        ch.step(nc.vector.reduce_max(code32[:, 0:1], n_kept[:, :], AX))
                        ch.step(nc.vector.tensor_tensor(cut[:, :], cut[:, :], rcp_tied[:, :], ALU.mult))
                        ch.step(nc.vector.reciprocal(kept_sum[:, :], kept_sum[:, :]))
                        ch.join()
                        ch.step(nc.vector.transpose(code_t[:, :], code32[:, :]))
                        ch.step(nc.vector.tensor_scalar(a_rcp[:, 2 * half:2 * half + 2], kept_sum[:, :],
                                                        1.0 / (SE * SX), None, ALU.mult))
                        ch.join()
                        ch.step(nc.vector.reduce_max(code_i[:, :], code_t[:, :], AX))
                        ch.restart()

                    def codes():
                        parts = [dve.value_load(code_i[r:r + 1, 0:1], min_val=0, max_val=16) for r in range(0, P, 32)]
                        return parts[0] + parts[1] + parts[2] + parts[3]

                    def keep(q, half):
                        after(dve, y_ready, q * 2 - 2)
                        weigh(half)
                        with dve.While(lambda: codes() >= 16):
                            for k in range(2):
                                ch.step(nc.vector.tensor_scalar(hit[:, k:k + 1], hold[:, k:k + 1], -1.0, 1.0,
                                                                ALU.mult, ALU.add))
                                ch.join()
                                ch.step(nc.vector.tensor_tensor(hit[:, k:k + 1], hit[:, k:k + 1], thr[:, k:k + 1],
                                                                ALU.mult))
                                ch.join()
                                ch.step(nc.vector.tensor_tensor(thr[:, k:k + 1], hit[:, k:k + 1], edge[:, k:k + 1],
                                                                ALU.max))
                                ch.join()
                            locate(half, (0, 1))
                            ch.join()
                            weigh(half)
                        with dve.If(codes() >= 1):
                            for k in range(2):
                                slot = 2 * half + k
                                ch.step(nc.vector.tensor_scalar(e[:, slot, :], kept[:, k, :], edge[:, k:k + 1],
                                                                cut[:, k:k + 1], ALU.is_equal, ALU.mult))
                                ch.join()
                                ch.step(nc.vector.tensor_tensor(kept[:, k, :], kept[:, k, :], e[:, slot, :],
                                                                ALU.subtract))
                                ch.join()
                            ch.restart()
                        dve.sem_inc(kept_ready, 2)

                    for k in range(2):
                        maximum(k, k)
                    ch.restart()

                    def pair(q, half, before_last, last, this, after_this):
                        other = 1 - half
                        if this:
                            dve.wait_ge(exp_ready, q * 2 + 1)
                            tot = total[:, 2 * half:2 * half + 1]
                            ch.step(nc.vector.tensor_scalar(goal[:, 0:1], tot, TOP_P, None, ALU.mult))
                            ch.step(nc.vector.tensor_scalar(thr[:, 0:1], tot, lower_end * first_ratio, None, ALU.mult))
                            ch.join()
                        for h in range(halvings):
                            if this:
                                halve(2 * half, h)
                            if h == DVE_AT[0] and after_this:
                                maximum(q * 2 + 2, 2 * other)
                            if h == DVE_AT[1]:
                                if last:
                                    a_low(q * 2 - 2)
                                if this:
                                    r_out(q, 0)
                            if h == 2 and final and before_last:
                                for k in range(2):
                                    normalise(q, k)
                            if h == DVE_AT[2] and last:
                                y_out(q, 0, 2 * other)
                        if this:
                            locate(half, (0,))
                        if after_this:
                            maximum(q * 2 + 3, 2 * other + 1)
                        if last:
                            a_low(q * 2 - 1)
                        if this:
                            r_out(q, 1)
                            dve.wait_ge(thr_final, q + 1)
                            locate(half, (1,))
                            ch.join()
                        if last:
                            y_out(q, 1, 2 * other + 1)
                        if this:
                            keep(q, half)
                        ch.restart()
                    skewed(dve, pair)

        stage_norm()
        for p in range(2):
            stage_project(p)
            stage_multiply(p)


def kernel(x, adj, L0_gnn_W1, L0_gnn_W2, L0_gnn_W3, L0_gnn_U1_0, L0_gnn_U1_1, L0_gnn_U2_0, L0_gnn_U2_1,
           L0_gnn_gamma, L0_gnn_beta):
    import numpy as np
    import concourse.bacc as bacc
    from concourse.bass_utils import run_bass_kernel_spmd

    n = x.shape[0]
    adj_t = np.ascontiguousarray(np.asarray(adj).reshape(n // P, P, n // P, P).transpose(0, 3, 2, 1))
    given = {
        "x": x, "adj_t": adj_t.reshape(n // P, P, n), "w1_t": np.asarray(L0_gnn_W1).T, "w2": L0_gnn_W2,
        "w3": L0_gnn_W3, "u1_0": L0_gnn_U1_0, "u1_1": L0_gnn_U1_1, "u2_0": L0_gnn_U2_0, "u2_1": L0_gnn_U2_1,
        "gamma": L0_gnn_gamma, "beta": L0_gnn_beta,
    }
    nc = bacc.Bacc("TRN2", target_bir_lowering=False, num_devices=1)
    arrays, args = {}, []
    for name, a in given.items():
        arrays[name] = np.ascontiguousarray(a)
        args.append(nc.dram_tensor(name, arrays[name].shape, mybir.dt.from_np(arrays[name].dtype),
                                   kind="ExternalInput").ap())
    args.append(nc.dram_tensor("out", x.shape, F32, kind="ExternalOutput").ap())
    gnn_layer(nc, *args)
    return run_bass_kernel_spmd(nc, [arrays], core_ids=[0]).results[0]["out"]
```

```python
import concourse.bass as bass
from concourse import mybir
from contextlib import ExitStack

F32 = mybir.dt.float32
F16 = mybir.dt.float16
I32 = mybir.dt.int32
U8 = mybir.dt.uint8
ALU = mybir.AluOpType
ACT = mybir.ActivationFunctionType
AX = mybir.AxisListType.X

P = 128
TOP_P = 0.9
LN_EPS = 1e-5

SX = 64.0
SW = 64.0
SE = 1024.0
SQ = 32.0

HALVINGS = (7, 11)
ROUND = 12582912.0
SLACK = 1e-5


ACT_AFTER = (
    {1: (("a_high", 0, (0, 1)), ("a_high", 0, (2, 3))), 2: (("exp", 0),), 3: (("s_high", 1),),
     4: (("a_high", 1, (0, 1)), ("y", 0), ), 5: (("a_high", 1, (2, 3)), ("exp", 1)), 6: (("s_high", 0),),
     7: (("y_high", 0), ("y", 1), ("y_high", 1))},
    {3: (("a_high", 0, (0, 1)), ("a_high", 0, (2, 3))), 4: (("exp", 0), ("s_high", 1)),
     6: (("a_high", 1, (0, 1)),), 7: (("exp", 1), ("a_high", 1, (2, 3))), 9: (("s_high", 0),)})
DVE_AFTER = (
    {0: (("a_low", 0, (0, 1)), ("s_sum", 0)), 1: (("a_low", 0, (2, 3)), ("max", 0)), 2: (("r_out_last", 1),),
     5: (("a_low", 1, (0, 1)),), 6: (("a_low", 1, (2, 3)), ("max", 1)), 7: (("r_out", 0), ("s_sum", 1)),
     8: (("y_low", 0), ("y_low", 1))},
    {0: (("a_low", 0, (0, 1)),), 1: (("a_low", 0, (2, 3)), ("max", 0)), 3: (("normalise", 0), ("normalise", 1)),
     6: (("a_low", 1, (0, 1)), ("max", 1)), 7: (("a_low", 1, (2, 3)),("y_sum", 0)), 11: (("r_out", 0), ),
     12: (("y_sum", 1),("r_out", 1), )})
POOL_AFTER = (
    {3: (("s_low", 1, (0, 1)),), 4: (("s_low", 1, (2, 3)),), 6: (("s_low", 0, (0, 1, 2, 3)),)},
    {4: (("rstd", 0), ("rstd", 1),("s_low", 1, (0, 1))),
     5: (("scale", 0),("s_low", 1, (2, 3))), 6: (("shift", 0),), 7: (("add", 0), ("scale", 1)), 8: (("shift", 1),),
     9: (("add", 1), ("s_low", 0, (0, 1))), 10: (("s_low", 0, (2, 3)),)})


def bracket_steps(n_cols, halvings):
    span = (n_cols / (1.0 - TOP_P)) * 1.05
    ratio = [span ** (0.5 ** (k + 1)) for k in range(halvings)]
    steps = [(ratio[k + 1] - ratio[k + 1] / ratio[k], ratio[k + 1] / ratio[k]) for k in range(halvings - 1)]
    up = 1.0 + 2.0 ** -17
    return ratio[0], steps + [((ratio[-1] - 1.0) * up, up)]


class Chain:

    def __init__(self, eng, sem):
        self.eng, self.sem, self.n = eng, sem, 0

    def step(self, ins):
        ins.then_inc(self.sem, 1)
        self.n += 1

    def join(self):
        self.eng.wait_ge(self.sem, self.n)

    def restart(self):
        if self.n:
            self.join()
            self.eng.sem_clear(self.sem)
            self.n = 0


def gnn_layer(nc, x, adj_t, w1_t, w2, w3, u1_0, u1_1, u2_0, u2_1, gamma, beta, out):
    N, D = x.shape
    DA = w2.shape[0]
    NT, DT = N // P, D // P
    CH = 512
    NC = N // CH
    NPAIR = NT // 2
    BLK = CH // P
    lower_end = (1.0 - TOP_P) / N * (1.0 - 2.0 ** -12)

    ctx = ExitStack()
    with ctx:
        def sb(name, shape, dt=F32):
            return ctx.enter_context(nc.sbuf_tensor(name, shape, dt))

        def ps(name, shape, dt=F32):
            return ctx.enter_context(nc.psum_tensor(name, shape, dt))

        def sem(name):
            return ctx.enter_context(nc.semaphore(name))

        def split(name, shape):
            return sb(name + "_hi", shape, F16), sb(name + "_lo", shape, F16)

        h_dram = nc.dram_tensor("h_scratch", [NT, P, D], F32, kind="Internal")
        base_dram = [nc.dram_tensor(f"base_scratch{p}", [NT, P, D], F32, kind="Internal") for p in range(2)]
        v_dram = nc.dram_tensor("v_scratch", [NT, P, D], F32, kind="Internal")

        mov_hi, mov_lo = split("mov", [P, NT, D])
        feat_hi, feat_lo = split("feat_t", [P, DT, N])
        vec_hi, vec_lo = split("vec", [P, NT, D])
        e = sb("e", [P, 4, N])
        kept = sb("kept", [P, 2, N])
        scrap = sb("scrap", [P, 3, N], U8)
        at_hi, at_lo = split("a_t", [P, NT, P])
        s_in = sb("s_in", [P, N])
        s_hi, s_lo = split("s", [P, 2, N])
        query = sb("query", [P, N], F16)
        key_hi, key_lo = split("key", [P, N])
        row_in = sb("row_in", [P, 2, D])
        y_row = sb("y_row", [P, 2, D])
        ident = sb("ident", [P, P])
        ident_h = sb("ident_h", [P, P], F16)
        ones_h = sb("ones_h", [P, 1], F16)
        small = sb("small", [P, 160])
        taken = [0]

        def columns(n):
            taken[0] += n
            return small[:, taken[0] - n:taken[0]]

        stats = sb("stats", [P, 2, 6])
        mean_var = sb("mean_var", [P, 2, 2])
        rstd = columns(2)
        shift = columns(2)
        half_col = columns(1)
        goal_col = columns(1)
        minus_col = columns(1)
        row_max = columns(4)
        neg_max = columns(4)
        total = columns(4)
        s_rcp = columns(NT)
        a_rcp = columns(4)
        goal = columns(4)
        thr = columns(4)
        above = columns(2)
        hit = columns(2)
        under = columns(2)
        top8 = sb("top8", [P, 2, 8])
        cum8 = sb("cum8", [P, 2, 8])
        reached8 = sb("reached8", [P, 2, 8])
        edge = columns(2)
        sum_ge = columns(2)
        sum_gt = columns(2)
        rcp_edge = columns(2)
        n_tied = columns(2)
        n_kept = columns(2)
        cut = columns(2)
        kept_sum = columns(2)
        rcp_tied = columns(2)
        ones8 = columns(8)
        n_col = columns(1)
        neg_thr = columns(1)
        next_thr = columns(1)
        excess = columns(1)
        signs = columns(1)
        reach = columns(1)
        hold = columns(2)
        code32 = columns(32)
        code_t = columns(32)
        code_4 = columns(4)
        assert taken[0] <= 160, taken
        code_i = sb("code_i", [P, 1], I32)

        ua = [s[:, 0, :].rearrange("p (t n) -> p t n", t=DT) for s in (s_hi, s_lo)]
        ub = [s[:, 1, :].rearrange("p (t n) -> p t n", t=DT) for s in (s_hi, s_lo)]
        u_raw = [e[:, k, :].rearrange("p (t n) -> p t n", t=DT) for k in range(2)]
        qk_w = sb("qk_w", [P, 2, 2, DT, P], F16)
        w_hi, w_lo = qk_w[:, 0], qk_w[:, 1]
        last_rows = qk_w[:, :].rearrange("p a b c d -> p (a b c d)").bitcast(F32)
        gamma_b, beta_b = last_rows[:, 0:D], last_rows[:, D:2 * D]
        wk_raw = e[:, 2, 0:DT * P].rearrange("p (t n) -> p t n", t=DT)
        w1_raw = e[0:DA, 2, DT * P:DT * P + D]
        w2_raw = e[0:DA, 2, DT * P + D:DT * P + D + P]

        r_rows = [f[:, :, :].rearrange("p d n -> p (d n)").bitcast(F32).rearrange("p (q n) -> p q n", n=D)
                  for f in (feat_hi, feat_lo)]

        logits = ps("logits", [P, N])
        turn = ps("turn", [P, 2, CH])
        acc_a = ps("acc_a", [P, CH])
        acc_r = ps("acc_r", [P, CH])

        def split_hi(dst, src, scale):
            return nc.scalar.activation(dst, src, ACT.Copy, scale=scale)

        def split_lo(dst, src, hi, scale):
            return nc.vector.scalar_tensor_tensor(out=dst, in0=src, scalar=scale, in1=hi,
                                                  op0=ALU.mult, op1=ALU.subtract)

        def product3(psum, left, right, count, opens=True):
            for k in range(count):
                l_hi, l_lo, r_hi, r_lo = left(0, k), left(1, k), right(0, k), right(1, k)
                nc.tensor.matmul(psum, l_hi, r_hi, start=(opens and k == 0), stop=False)
                nc.tensor.matmul(psum, l_hi, r_lo, start=False, stop=False)
                last = nc.tensor.matmul(psum, l_lo, r_hi, start=False,
                                        stop=(k == count - 1))
            return last

        def cols(t):
            return bass.ds(t * P, P)

        def plane(tile3, t):
            return tile3[:, bass.ds(t, 1), :].rearrange("p a d -> p (a d)")

        def dram_rows(tensor, t):
            return tensor[bass.ds(t, 1), :, :].rearrange("a p d -> p (a d)")

        def after(eng, semaphore, value):
            if not isinstance(value, int) or value > 0:
                eng.wait_ge(semaphore, value)

        def by_pairs(eng, body):
            body(0)
            with eng.Fori(1, NPAIR) as q:
                body(q)

        def stage_norm():
            const_ready = sem("const_ready")
            gp_step = sem("gp_step")
            w_loaded = sem("w_loaded")
            x_loaded = [sem(f"x_loaded{k}") for k in range(2)]
            var_ready = sem("var_ready")
            rstd_ready = sem("rstd_ready")
            shift_ready = sem("shift_ready")
            h_ready = sem("h_ready")
            h_hi_ready = sem("h_hi_ready")
            h_lo_ready = sem("h_lo_ready")
            h_turned = sem("h_turned")
            ft_hi_ready = sem("ft_hi_ready")
            ft_lo_ready = sem("ft_lo_ready")
            h_stored = [sem(f"h_stored{k}") for k in range(2)]
            w12_ready = sem("w12_ready")
            w_hi_ready = sem("w_hi_ready")
            dve_step = sem("norm_dve_step")

            with nc.Block() as block:
                @block.sync
                def _(sp):
                    w3_rows = w3.rearrange("(t p) n -> p t n", p=P)
                    sp.dma_start(w1_raw, w1_t).then_inc(w_loaded, 16)
                    sp.dma_start(w2_raw[:, 0:DA], w2).then_inc(w_loaded, 16)
                    sp.dma_start(w2_raw[:, DA:P], w2).then_inc(w_loaded, 16)
                    sp.dma_start(wk_raw[:, :, 0:DA], w3_rows).then_inc(w_loaded, 16)
                    sp.dma_start(wk_raw[:, :, DA:P], w3_rows).then_inc(w_loaded, 16)

                    def pair(q):
                        for k in range(2):
                            t = q * 2 + k
                            after(sp, h_ready, t - 1)
                            sp.dma_start(row_in[:, k, :], x[cols(t), :]).then_inc(x_loaded[k], 16)
                        for k in range(2):
                            t = q * 2 + k
                            sp.wait_ge(h_ready, t + 1)
                            sp.dma_start(dram_rows(h_dram, t), y_row[:, k, :]).then_inc(h_stored[k], 16)
                    by_pairs(sp, pair)
                    sp.wait_ge(w_loaded, 16 * 5)
                    for k in range(2):
                        sp.wait_ge(h_stored[k], 16 * NPAIR)

                @block.gpsimd
                def _(gp):
                    nc.gpsimd.memset(ident[:, :], 0.0).then_inc(gp_step, 1)
                    nc.gpsimd.memset(half_col[:, :], -0.5).then_inc(gp_step, 1)
                    gp.wait_ge(gp_step, 2)
                    nc.gpsimd.affine_select(out=ident[:, :], in_=ident[:, :], compare_op=ALU.not_equal, fill=1.0,
                                            base=0, pattern=[[-1, P]], channel_multiplier=1).then_inc(gp_step, 1)
                    gp.wait_ge(gp_step, 3)
                    nc.gpsimd.tensor_copy(ident_h[:, :], ident[:, :]).then_inc(const_ready, 1)
                    nc.gpsimd.memset(ones_h[:, :], 1.0)
                    nc.gpsimd.memset(ones8[:, :], 1.0)
                    nc.gpsimd.memset(minus_col[:, :], -1.0)
                    nc.gpsimd.memset(goal_col[:, :], TOP_P)
                    nc.gpsimd.memset(n_col[:, :], float(N))
                    nc.gpsimd.memset(code32[:, :], 0.0)

                    def pair(q):
                        for k in range(2):
                            t = q * 2 + k
                            gp.wait_ge(var_ready, t + 1)
                            after(gp, h_ready, t - 1)
                            nc.gpsimd.tensor_tensor(rstd[:, k:k + 1], mean_var[:, k, 1:2], half_col[:, :],
                                                    ALU.pow).then_inc(rstd_ready, 1)
                    by_pairs(gp, pair)

                @block.vector
                def _(dve):
                    ch = Chain(dve, dve_step)
                    nc.vector.memset(key_lo[:, :], 0.0)
                    dve.wait_ge(w_hi_ready, 1)
                    split_lo(w_lo[:, 0].rearrange("p t n -> p (t n)"), acc_a[:, :],
                             w_hi[:, 0].rearrange("p t n -> p (t n)"), SW)
                    dve.wait_ge(w_hi_ready, 2)
                    split_lo(w_lo[:, 1], wk_raw, w_hi[:, 1], SW)

                    def pair(q):
                        for k in range(2):
                            t = q * 2 + k
                            after(dve, rstd_ready, t - 1)
                            after(dve, shift_ready, t - 1)
                            dve.wait_ge(x_loaded[k], (q + 1) * 16)
                            ch.step(nc.vector.bn_stats(stats[:, k, :], row_in[:, k, :]))
                            ch.join()
                            ch.step(nc.vector.bn_aggr(mean_var[:, k, :], stats[:, k, :]))
                            ch.join()
                            nc.vector.tensor_scalar(mean_var[:, k, 1:2], mean_var[:, k, 1:2], LN_EPS, None,
                                                    ALU.add).then_inc(var_ready, 1)
                        for k in range(2):
                            t = q * 2 + k
                            dve.wait_ge(rstd_ready, t + 1)
                            after(dve, h_ready, t - 1)
                            nc.vector.scalar_tensor_tensor(out=shift[:, k:k + 1], in0=mean_var[:, k, 0:1], scalar=-1.0,
                                                           in1=rstd[:, k:k + 1], op0=ALU.mult,
                                                           op1=ALU.mult).then_inc(shift_ready, 1)
                        for k in range(2):
                            t = q * 2 + k
                            dve.wait_ge(h_hi_ready, t + 1)
                            split_lo(plane(mov_lo, t), y_row[:, k, :], plane(mov_hi, t), SX).then_inc(h_lo_ready, 1)
                            dve.wait_ge(ft_hi_ready, t + 1)
                            split_lo(feat_lo[:, :, cols(t)], turn[:, k, :].rearrange("p (d n) -> p d n", d=DT),
                                     feat_hi[:, :, cols(t)], SX).then_inc(ft_lo_ready, 1)
                        ch.restart()
                    by_pairs(dve, pair)

                @block.scalar
                def _(act):
                    act.wait_ge(w12_ready, 1)
                    split_hi(w_hi[:, 0].rearrange("p t n -> p (t n)"), acc_a[:, :], SW).then_inc(w_hi_ready, 1)
                    act.wait_ge(w_loaded, 16 * 5)
                    split_hi(w_hi[:, 1], wk_raw, SW).then_inc(w_hi_ready, 1)

                    def pair(q):
                        for k in range(2):
                            t = q * 2 + k
                            act.wait_ge(shift_ready, t + 1)
                            after(act, h_stored[k], q * 16)
                            after(act, h_lo_ready, t - 1)
                            after(act, h_turned, t - 1)
                            nc.scalar.activation(y_row[:, k, :], row_in[:, k, :], ACT.Relu, bias=shift[:, k:k + 1],
                                                 scale=rstd[:, k:k + 1]).then_inc(h_ready, 1)
                        for k in range(2):
                            t = q * 2 + k
                            act.wait_ge(h_ready, t + 1)
                            split_hi(plane(mov_hi, t), y_row[:, k, :], SX).then_inc(h_hi_ready, 1)
                            act.wait_ge(h_turned, t + 1)
                            split_hi(feat_hi[:, :, cols(t)], turn[:, k, :].rearrange("p (d n) -> p d n", d=DT),
                                     SX).then_inc(ft_hi_ready, 1)
                    by_pairs(act, pair)

                @block.tensor
                def _(pe):
                    pe.wait_ge(w_loaded, 16 * 5)
                    for d in range(DT):
                        last = nc.tensor.matmul(acc_a[:, d * P:(d + 1) * P], w1_raw[:, d * P:(d + 1) * P], w2_raw,
                                                start=True, stop=True)
                    last.then_inc(w12_ready, 1)
                    pe.wait_ge(const_ready, 1)

                    def pair(q):
                        for k in range(2):
                            t = q * 2 + k
                            pe.wait_ge(h_ready, t + 1)
                            after(pe, ft_lo_ready, t - 1)
                            for d in range(DT):
                                last = nc.tensor.transpose(turn[:, k, d * P:(d + 1) * P],
                                                           y_row[:, k, d * P:(d + 1) * P], ident[:, :])
                            last.then_inc(h_turned, 1)
                    by_pairs(pe, pair)

        def stage_project(p):
            w_a, w_b = ((u1_1, u1_0), (u2_1, u2_0))[p]
            dst_hi, dst_lo = ((vec_hi, vec_lo), (mov_hi, mov_lo))[p]
            u_loaded = sem(f"u_loaded{p}")
            u_hi_ready = sem(f"u_hi_ready{p}")
            u_lo_ready = sem(f"u_lo_ready{p}")
            qk_done = sem(f"qk_done{p}")
            qk_hi_ready = sem(f"qk_hi_ready{p}")
            qk_lo_ready = sem(f"qk_lo_ready{p}")
            prod_done = sem(f"prod_done{p}")
            dst_hi_ready = sem(f"dst_hi_ready{p}")
            dst_lo_ready = sem(f"dst_lo_ready{p}")
            base_ready = sem(f"base_ready{p}")
            base_stored = [sem(f"base_stored{p}_{k}") for k in range(2)]
            h_loaded = [sem(f"h_loaded{p}_{k}") for k in range(2)]
            v_loaded = [sem(f"v_loaded{p}_{k}") for k in range(2)]
            v_hi_ready = sem(f"v_hi_ready{p}")
            v_lo_ready = sem(f"v_lo_ready{p}")

            with nc.Block() as block:
                @block.sync
                def _(sp):
                    for k, w in enumerate((w_a, w_b)):
                        sp.dma_start(u_raw[k], w.rearrange("(t p) n -> p t n", p=P)).then_inc(u_loaded, 16)

                    def pair(q):
                        if p == 1:
                            for k in range(2):
                                t = q * 2 + k
                                after(sp, base_stored[k], q * 16)
                                sp.dma_start(row_in[:, k, :], dram_rows(h_dram, t)).then_inc(h_loaded[k], 16)
                                after(sp, v_lo_ready, t - 1)
                                sp.dma_start(y_row[:, k, :], dram_rows(v_dram, t)).then_inc(v_loaded[k], 16)
                        for k in range(2):
                            t = q * 2 + k
                            sp.wait_ge(base_ready, t + 1)
                            sp.dma_start(dram_rows(base_dram[p], t), row_in[:, k, :]).then_inc(base_stored[k], 16)
                    by_pairs(sp, pair)
                    for k in range(2):
                        sp.wait_ge(base_stored[k], 16 * NPAIR)

                @block.tensor
                def _(pe):
                    for c in range(NC):
                        for w in range(2):
                            after(pe, qk_lo_ready, 2 * c + w - 1)
                            product3(turn[:, w, :], lambda part, d: (w_hi, w_lo)[part][:, w, d, :],
                                     lambda part, d: (feat_hi, feat_lo)[part][:, d, c * CH:(c + 1) * CH],
                                     DT).then_inc(qk_done, 1)
                    pe.wait_ge(u_lo_ready, 2)

                    def pair(q):
                        for k in range(2):
                            t = q * 2 + k
                            for w, u in enumerate((ua, ub)):
                                after(pe, (dst_lo_ready, base_ready)[w], t - 1)
                                bank = 2 * w + k
                                product3(logits[:, bank * CH:(bank + 1) * CH],
                                         lambda part, d: (feat_hi, feat_lo)[part][:, d, cols(t)],
                                         lambda part, d: u[part][:, d, :], DT).then_inc(prod_done, 1)
                    by_pairs(pe, pair)

                @block.scalar
                def _(act):
                    act.wait_ge(u_loaded, 32)
                    for k, u in enumerate((ua, ub)):
                        split_hi(u[0], u_raw[k], SW).then_inc(u_hi_ready, 1)
                    for c in range(NC):
                        for w in range(2):
                            act.wait_ge(qk_done, 2 * c + w + 1)
                            split_hi((query, key_hi)[w][:, c * CH:(c + 1) * CH], turn[:, w, :],
                                     SQ / (SX * SW)).then_inc(qk_hi_ready, 1)

                    def pair(q):
                        for k in range(2):
                            t = q * 2 + k
                            act.wait_ge(prod_done, t * 2 + 1)
                            split_hi(plane(dst_hi, t), logits[:, k * CH:(k + 1) * CH],
                                     1.0 / SW).then_inc(dst_hi_ready, 1)
                            if p == 1:
                                act.wait_ge(v_loaded[k], (q + 1) * 16)
                                split_hi(plane(vec_hi, t), y_row[:, k, :], SX).then_inc(v_hi_ready, 1)
                    by_pairs(act, pair)

                @block.vector
                def _(dve):
                    for k, u in enumerate((ua, ub)):
                        dve.wait_ge(u_hi_ready, k + 1)
                        split_lo(u[1], u_raw[k], u[0], SW).then_inc(u_lo_ready, 1)
                    for c in range(NC):
                        for w in range(2):
                            dve.wait_ge(qk_hi_ready, 2 * c + w + 1)
                            lo, hi = ((DA, P), (0, DA))[w]
                            span = slice(c * CH, (c + 1) * CH)
                            split_lo((query, key_lo)[w][lo:hi, span], turn[lo:hi, w, :],
                                     (query, key_hi)[w][lo:hi, span], SQ / (SX * SW)).then_inc(qk_lo_ready, 1)

                    def pair(q):
                        for k in range(2):
                            t = q * 2 + k
                            dve.wait_ge(dst_hi_ready, t + 1)
                            split_lo(plane(dst_lo, t), logits[:, k * CH:(k + 1) * CH], plane(dst_hi, t),
                                     1.0 / SW).then_inc(dst_lo_ready, 1)
                            dve.wait_ge(prod_done, t * 2 + 2)
                            after(dve, base_stored[k], q * 16)
                            bank = logits[:, (2 + k) * CH:(3 + k) * CH]
                            if p == 0:
                                nc.vector.tensor_scalar(row_in[:, k, :], bank, 1.0 / (SX * SW), None,
                                                        ALU.mult).then_inc(base_ready, 1)
                            else:
                                dve.wait_ge(h_loaded[k], (q + 1) * 16)
                                nc.vector.scalar_tensor_tensor(
                                    out=row_in[:, k, :], in0=bank, scalar=1.0 / (SX * SW), in1=row_in[:, k, :],
                                    op0=ALU.mult, op1=ALU.add).then_inc(base_ready, 1)
                                dve.wait_ge(v_hi_ready, t + 1)
                                split_lo(plane(vec_lo, t), y_row[:, k, :], plane(vec_hi, t),
                                         SX).then_inc(v_lo_ready, 1)
                    by_pairs(dve, pair)

        def stage_multiply(p):
            final = p == 1
            halvings = HALVINGS[p]
            first_ratio, steps = bracket_steps(N, halvings)
            s_loaded = sem(f"s_loaded{p}")
            s_hi_ready = sem(f"s_hi_ready{p}")
            s_lo_ready = sem(f"s_lo_ready{p}")
            base_loaded = [sem(f"base_loaded{p}_{k}") for k in range(2)]
            logits_done = sem(f"logits_done{p}")
            max_ready = sem(f"max_ready{p}")
            exp_ready = sem(f"exp_ready{p}")
            kept_ready = sem(f"kept_ready{p}")
            a_turned = sem(f"a_turned{p}")
            at_hi_ready = sem(f"at_hi_ready{p}")
            at_lo_ready = sem(f"at_lo_ready{p}")
            s_sum_done = sem(f"s_sum_done{p}")
            s_rcp_ready = sem(f"s_rcp_ready{p}")
            r_done = sem(f"r_done{p}")
            r_read = sem(f"r_read{p}")
            a_done = sem(f"a_done{p}")
            y_ready = sem(f"y_ready{p}")
            search_step = sem(f"search_step{p}")
            thr_set = sem(f"thr_set{p}")
            sums_ready = sem(f"sums_ready{p}")
            thr_final = sem(f"thr_final{p}")
            update_step = sem(f"update_step{p}")
            if final:
                last_loaded = sem("last_loaded")
                x_loaded = [sem(f"last_x_loaded{k}") for k in range(2)]
                var_ready = sem("last_var_ready")
                rstd_ready = sem("last_rstd_ready")
                normed = sem("normed")
                out_stored = [sem(f"out_stored{k}") for k in range(2)]
            else:
                y_turned = sem("y_turned")
                y_hi_ready = sem("y_hi_ready")
                y_lo_ready = sem("y_lo_ready")
                v_stored = [sem(f"v_stored{k}") for k in range(2)]

            def skewed(eng, body):
                body(0, 0, False, False, True, True)
                body(1, 1, False, True, True, True)
                with eng.Fori(1, NPAIR // 2 - 1) as i:
                    body(i * 2, 0, True, True, True, True)
                    body(i * 2 + 1, 1, True, True, True, True)
                body(NPAIR - 2, 0, True, True, True, True)
                body(NPAIR - 1, 1, True, True, True, False)
                body(NPAIR, 0, True, True, False, False)
                if final:
                    body(NPAIR + 1, 1, True, False, False, False)

            with nc.Block() as block:
                @block.sync
                def _(sp):
                    def load_s(t):
                        after(sp, s_lo_ready, t)
                        sp.dma_start(s_in[:, :], adj_t[bass.ds(t, 1), :, :].rearrange("a p n -> p (a n)")
                                     ).then_inc(s_loaded, 16)

                    def load_base(t, k):
                        sp.dma_start(row_in[:, k, :], dram_rows(base_dram[p], t)).then_inc(base_loaded[k], 16)

                    def row_used(q, k, more):
                        sp.wait_ge(r_read, q * 2 + k + 1)
                        if not final:
                            sp.dma_start(dram_rows(v_dram, q * 2 + k), row_in[:, k, :]).then_inc(v_stored[k], 16)
                            sp.wait_ge(v_stored[k], (q + 1) * 16)
                        if more:
                            load_base(q * 2 + 2 + k, k)

                    load_s(0)
                    for k in range(2):
                        load_base(k, k)
                    if final:
                        for dst, row in ((gamma_b, gamma), (beta_b, beta)):
                            sp.dma_start(dst, row.rearrange("(a d) -> a d", a=1).to_broadcast([P, D])
                                         ).then_inc(last_loaded, 16)

                    def pair(q, half, before_last, last, this, after_this):
                        if this:
                            load_s(q * 2 + 1)
                        if last:
                            row_used(q - 1, 1, this)
                        if after_this:
                            load_s(q * 2 + 2)
                        if this:
                            row_used(q, 0, after_this)
                    skewed(sp, pair)
                    if final:
                        sp.wait_ge(last_loaded, 32)
                    else:
                        for k in range(2):
                            sp.wait_ge(v_stored[k], 16 * NPAIR)

                @block.gpsimd
                def _(gp):
                    if final:
                        gp.wait_ge(last_loaded, 32)

                    ch = Chain(gp, update_step)

                    def s_low(t, slot, chunks):
                        gp.wait_ge(s_hi_ready, t + 1)
                        for c in chunks:
                            span = slice(c * CH, (c + 1) * CH)
                            ins = nc.gpsimd.tensor_tensor(s_lo[:, slot, span], s_in[:, span], s_hi[:, slot, span],
                                                          ALU.subtract)
                            if c == NC - 1:
                                ins.then_inc(s_lo_ready, 1)

                    s_low(0, 0, range(NC))

                    def start_second(q, half):
                        tot = total[:, 2 * half + 1:2 * half + 2]
                        gp.wait_ge(exp_ready, q * 2 + 2)
                        ch.step(nc.gpsimd.tensor_tensor(goal[:, 2 * half + 1:2 * half + 2], tot, goal_col[:, :], ALU.mult))
                        ch.step(nc.gpsimd.tensor_scalar(neg_thr[:, :], tot, -lower_end * first_ratio, None, ALU.mult))
                        ch.join()
                        gp.sem_inc(thr_set, 1)

                    def halve_second(q, half, h):
                        gain, miss = steps[h]
                        ch.step(nc.gpsimd.tensor_scalar(next_thr[:, :], neg_thr[:, :], gain, None, ALU.mult))
                        gp.wait_ge(sums_ready, q * (2 * halvings) + 2 * h + 2)
                        ch.step(nc.gpsimd.tensor_tensor(reach[:, :], signs[:, :], n_col[:, :], ALU.add))
                        ch.join()
                        ch.step(nc.gpsimd.tensor_scalar(reach[:, :], reach[:, :], -0.5, neg_thr[:, :],
                                                        ALU.mult, ALU.mult))
                        ch.join()
                        ch.step(nc.gpsimd.tensor_scalar(reach[:, :], reach[:, :], excess[:, :],
                                                        goal[:, 2 * half + 1:2 * half + 2],
                                                        ALU.add, ALU.is_ge))
                        ch.join()
                        ch.step(nc.gpsimd.tensor_scalar(neg_thr[:, :], reach[:, :], miss / gain, next_thr[:, :],
                                                        ALU.add, ALU.mult))
                        ch.join()
                        if h < halvings - 1:
                            gp.sem_inc(thr_set, 1)
                        else:
                            ch.step(nc.gpsimd.tensor_tensor(thr[:, 2 * half + 1:2 * half + 2], neg_thr[:, :],
                                                            minus_col[:, :], ALU.mult))
                            ch.join()
                            gp.sem_inc(thr_final, 1)

                    def finish_row(q, k, part):
                        t = q * 2 - 4 + k
                        y, r_part = y_row[:, k, :], plane(r_rows[k], q - 2)
                        if part == "rstd":
                            gp.wait_ge(var_ready, t + 1)
                            ch.step(nc.gpsimd.tensor_tensor(rstd[:, k:k + 1], mean_var[:, k, 1:2], half_col[:, :],
                                                            ALU.pow))
                            ch.join()
                            gp.sem_inc(rstd_ready, 1)
                            gp.dma_start(r_part, x[cols(t), :]).then_inc(x_loaded[k], 16)
                        if part == "scale":
                            gp.wait_ge(normed, t + 1)
                            ch.step(nc.gpsimd.tensor_tensor(y, y, gamma_b, ALU.mult))
                            ch.join()
                        if part == "shift":
                            gp.wait_ge(x_loaded[k], (q - 1) * 16)
                            ch.step(nc.gpsimd.tensor_tensor(y, y, beta_b, ALU.add))
                            ch.join()
                        if part == "add":
                            ch.step(nc.gpsimd.tensor_tensor(y, y, r_part, ALU.add))
                            ch.join()
                            gp.dma_start(out[cols(t), :], y).then_inc(out_stored[k], 16)

                    def pair(q, half, before_last, last, this, after_this):
                        if this:
                            start_second(q, half)
                        for h in range(halvings):
                            if this:
                                halve_second(q, half, h)
                            for what, k, *chunks in POOL_AFTER[p].get(h, ()):
                                if what != "s_low":
                                    if before_last:
                                        finish_row(q, k, what)
                                elif (after_this, this)[k]:
                                    s_low(q * 2 + 2 - k, k, *chunks)
                        ch.restart()
                    skewed(gp, pair)
                    if final:
                        for k in range(2):
                            gp.wait_ge(out_stored[k], 16 * NPAIR)

                @block.scalar
                def _(act):
                    def s_high(t, slot):
                        act.wait_ge(s_loaded, t * 16 + 16)
                        after(act, r_done, t - 1)
                        split_hi(s_hi[:, slot, :], s_in[:, :], 1.0).then_inc(s_hi_ready, 1)

                    def exponential(t, slot):
                        act.wait_ge(max_ready, t + 1)
                        after(act, kept_ready, t - 3)
                        nc.scalar.activation(e[:, slot, :], logits[:, :], ACT.Exp, bias=neg_max[:, slot:slot + 1],
                                             scale=1.0 / (SQ * SQ), accum_out=total[:, slot:slot + 1]
                                             ).then_inc(exp_ready, 1)

                    def evaluate(q, slot, h):
                        act.wait_ge(thr_set, q * halvings + h + 1)
                        nc.scalar.activation(scrap[:, 1, :], e[:, slot, :], ACT.Relu, bias=neg_thr[:, :],
                                             accum_out=excess[:, :]).then_inc(sums_ready, 1)
                        nc.scalar.activation(scrap[:, 2, :], e[:, slot, :], ACT.Sign, bias=neg_thr[:, :],
                                             accum_out=signs[:, :]).then_inc(sums_ready, 1)

                    def a_high(t, chunks):
                        after(act, a_done, t)
                        for c in chunks:
                            act.wait_ge(a_turned, t * BLK + c + 1)
                            split_hi(at_hi[:, c * BLK:(c + 1) * BLK, :],
                                     turn[:, c % 2, :].rearrange("p (b n) -> p b n", b=BLK), SE
                                     ).then_inc(at_hi_ready, 1)

                    def y_scaled(t, k, slot):
                        act.wait_ge(a_done, t + 1)
                        after(act, y_turned, t - 1)
                        nc.scalar.activation(y_row[:, k, :], acc_a[:, :], ACT.Copy,
                                             scale=a_rcp[:, slot:slot + 1]).then_inc(y_ready, 1)

                    def y_high(t, k):
                        act.wait_ge(y_turned, t + 1)
                        split_hi(feat_hi[:, :, cols(t)], turn[:, k, :].rearrange("p (d n) -> p d n", d=DT),
                                 SX).then_inc(y_hi_ready, 1)

                    s_high(0, 0)
                    for k in range(2):
                        exponential(k, k)

                    def pair(q, half, before_last, last, this, after_this):
                        other = 1 - half
                        for h in range(halvings + 1):
                            if this and h < halvings:
                                evaluate(q, 2 * half + 1, h)
                            for what, k, *chunks in ACT_AFTER[p].get(h, ()):
                                if what == "a_high" and last:
                                    a_high(q * 2 - 2 + k, *chunks)
                                if what == "exp" and after_this:
                                    exponential(q * 2 + 2 + k, 2 * other + k)
                                if what == "s_high" and (after_this, this)[k]:
                                    s_high(q * 2 + 2 - k, k)
                                if what == "y" and last:
                                    y_scaled(q * 2 - 2 + k, k, 2 * other + k)
                                if what == "y_high" and last:
                                    y_high(q * 2 - 2 + k, k)
                    skewed(act, pair)

                @block.tensor
                def _(pe):
                    def logits_of(t):
                        after(pe, exp_ready, t)
                        for c in range(NC):
                            span = slice(c * CH, (c + 1) * CH)
                            nc.tensor.matmul(logits[:, span], query[:, cols(t)], key_hi[:, span], start=True, stop=False)
                            done = nc.tensor.matmul(logits[:, span], query[:, cols(t)], key_lo[:, span],
                                                    start=False, stop=True)
                        done.then_inc(logits_done, 1)

                    for k in range(2):
                        logits_of(k)

                    def s_sum(t, k, y_read):
                        pe.wait_ge(s_lo_ready, t + 1)
                        after(pe, y_ready, y_read)
                        after(pe, s_rcp_ready, t)
                        for j in range(NT):
                            nc.tensor.matmul(acc_a[:, 0:1], s_hi[:, k, j * P:(j + 1) * P], ones_h[:, :],
                                             start=(j == 0), stop=False)
                            done = nc.tensor.matmul(acc_a[:, 0:1], s_lo[:, k, j * P:(j + 1) * P], ones_h[:, :],
                                                    start=False, stop=(j == NT - 1))
                        done.then_inc(s_sum_done, 1)

                    def r_product(t, k):
                        pe.wait_ge(s_lo_ready, t + 1)
                        parts = [part[:, k, :].rearrange("p (j n) -> p j n", j=NT) for part in (s_hi, s_lo)]
                        after(pe, r_read, t)
                        nc.tensor.matmul(acc_r[:, :], ident_h[:, :], plane(vec_hi, t), start=True, stop=False)
                        nc.tensor.matmul(acc_r[:, :], ident_h[:, :], plane(vec_lo, t), start=False, stop=False)
                        product3(acc_r[:, :], lambda part, j: parts[part][:, j, :],
                                 lambda part, j: (vec_hi, vec_lo)[part][:, j, :], NT,
                                 opens=False).then_inc(r_done, 1)

                    def turn_a(u, k, chunks):
                        pe.wait_ge(kept_ready, u + 1)
                        for c in chunks:
                            if c >= 2:
                                pe.wait_ge(at_lo_ready, u * BLK + c - 1)
                            elif k == 1 or final:
                                after(pe, at_lo_ready, u * BLK - 1 + c)
                            elif c == 0:
                                after(pe, y_lo_ready, u)
                            for b in range(BLK):
                                j = c * BLK + b
                                done = nc.tensor.transpose(turn[:, c % 2, b * P:(b + 1) * P],
                                                           kept[:, k, j * P:(j + 1) * P], ident[:, :])
                            done.then_inc(a_turned, 1)

                    def a_product(u, row_sums):
                        pe.wait_ge(at_lo_ready, (u + 1) * BLK)
                        after(pe, y_ready, u)
                        if row_sums is not None:
                            pe.wait_ge(s_rcp_ready, row_sums)
                        product3(acc_a[:, :], lambda part, j: (at_hi, at_lo)[part][:, j, :],
                                 lambda part, j: (mov_hi, mov_lo)[part][:, j, :], NT).then_inc(a_done, 1)

                    def turn_y(u, k):
                        if k == 0:
                            pe.wait_ge(at_lo_ready, (u + 1) * BLK + 3)
                        pe.wait_ge(y_ready, u + 1)
                        for d in range(DT):
                            done = nc.tensor.transpose(turn[:, k, d * P:(d + 1) * P],
                                                       y_row[:, k, d * P:(d + 1) * P], ident[:, :])
                        done.then_inc(y_turned, 1)

                    def pair(q, half, before_last, last, this, after_this):
                        t, u = q * 2, q * 2 - 2
                        first_sum, second_sum = (t + 1, t + 2) if this and not final else (None, None)
                        if last:
                            turn_a(u, 0, (0, 1))
                        if after_this:
                            logits_of(t + 2)
                        if this and not final:
                            s_sum(t, 0, u if last else 0)
                        if last:
                            turn_a(u, 0, (2, 3))
                            a_product(u, first_sum)
                            turn_a(u + 1, 1, (0, 1))
                        if after_this:
                            logits_of(t + 3)
                        if last:
                            turn_a(u + 1, 1, (2, 3))
                        if this:
                            r_product(t, 0)
                            if not final:
                                s_sum(t + 1, 1, u + 1 if last else 0)
                        if last:
                            if not final:
                                turn_y(u, 0)
                            a_product(u + 1, second_sum)
                            if not final:
                                turn_y(u + 1, 1)
                        if this:
                            r_product(t + 1, 1)
                    skewed(pe, pair)

                @block.vector
                def _(dve):
                    ch = Chain(dve, search_step)

                    def maximum(t, slot):
                        dve.wait_ge(logits_done, t + 1)
                        ch.step(nc.vector.reduce_max(row_max[:, slot:slot + 1], logits[:, :], AX))
                        ch.join()
                        nc.vector.tensor_scalar(neg_max[:, slot:slot + 1], row_max[:, slot:slot + 1],
                                                -1.0 / (SQ * SQ), None, ALU.mult).then_inc(max_ready, 1)

                    def a_low(t, chunks):
                        for c in chunks:
                            dve.wait_ge(at_hi_ready, t * BLK + c + 1)
                            split_lo(at_lo[:, c * BLK:(c + 1) * BLK, :],
                                     turn[:, c % 2, :].rearrange("p (b n) -> p b n", b=BLK),
                                     at_hi[:, c * BLK:(c + 1) * BLK, :], SE).then_inc(at_lo_ready, 1)

                    def s_sum(t):
                        rcp = s_rcp[:, bass.ds(t, 1)]
                        dve.wait_ge(s_sum_done, t + 1)
                        ch.step(nc.vector.tensor_scalar(rcp, acc_a[:, 0:1], 1.0, 1e-12, ALU.add, ALU.max))
                        ch.join()
                        ch.step(nc.vector.reciprocal(rcp, rcp))
                        ch.join()
                        ch.step(nc.vector.tensor_scalar(rcp, rcp, 1.0 / SX, None, ALU.mult))
                        ch.join()
                        dve.sem_inc(s_rcp_ready, 1)

                    def r_out(q, k):
                        t = q * 2 + k
                        dve.wait_ge(r_done, t + 1)
                        dve.wait_ge(base_loaded[k], (q + 1) * 16)
                        dst = plane(r_rows[k], q) if final else row_in[:, k, :]
                        nc.vector.scalar_tensor_tensor(out=dst, in0=acc_r[:, :], scalar=s_rcp[:, bass.ds(t, 1)],
                                                       in1=row_in[:, k, :],
                                                       op0=ALU.mult, op1=ALU.add).then_inc(r_read, 1)

                    def y_low(t, k):
                        dve.wait_ge(y_hi_ready, t + 1)
                        split_lo(feat_lo[:, :, cols(t)], turn[:, k, :].rearrange("p (d n) -> p d n", d=DT),
                                 feat_hi[:, :, cols(t)], SX).then_inc(y_lo_ready, 1)

                    def y_sum(q, k, slot):
                        t = q * 2 - 2 + k
                        dve.wait_ge(a_done, t + 1)
                        dve.wait_ge(r_read, t + 1)
                        after(dve, out_stored[k], (q - 1) * 16)
                        nc.vector.scalar_tensor_tensor(out=y_row[:, k, :], in0=acc_a[:, :],
                                                       scalar=a_rcp[:, slot:slot + 1], in1=plane(r_rows[k], q - 1),
                                                       op0=ALU.mult, op1=ALU.add).then_inc(y_ready, 1)
                        dve.wait_ge(y_ready, t + 1)
                        ch.step(nc.vector.bn_stats(stats[:, k, :], y_row[:, k, :]))
                        ch.join()
                        ch.step(nc.vector.bn_aggr(mean_var[:, k, :], stats[:, k, :]))
                        ch.join()
                        nc.vector.tensor_scalar(mean_var[:, k, 1:2], mean_var[:, k, 1:2], LN_EPS, None,
                                                ALU.add).then_inc(var_ready, 1)

                    def normalise(q, k):
                        dve.wait_ge(rstd_ready, q * 2 - 3 + k)
                        nc.vector.tensor_scalar(y_row[:, k, :], y_row[:, k, :], mean_var[:, k, 0:1], rstd[:, k:k + 1],
                                                ALU.subtract, ALU.mult).then_inc(normed, 1)

                    def halve(slot, h):
                        gain, miss = steps[h]
                        ch.step(nc.vector.scalar_tensor_tensor(
                            out=scrap[:, 0, :], in0=e[:, slot, :], scalar=thr[:, slot:slot + 1], in1=e[:, slot, :],
                            op0=ALU.is_gt, op1=ALU.mult, accum_out=above[:, 0:1]))
                        ch.join()
                        ch.step(nc.vector.tensor_scalar(hit[:, 0:1], above[:, 0:1], goal[:, slot:slot + 1], gain,
                                                        ALU.is_ge, ALU.mult))
                        ch.join()
                        ch.step(nc.vector.tensor_scalar(thr[:, slot:slot + 1], hit[:, 0:1], miss, thr[:, slot:slot + 1],
                                                        ALU.add, ALU.mult))
                        ch.join()

                    def locate(half, tiles):
                        for k in tiles:
                            slot = 2 * half + k
                            ch.step(nc.vector.scalar_tensor_tensor(
                                out=kept[:, k, :], in0=e[:, slot, :], scalar=thr[:, slot:slot + 1], in1=e[:, slot, :],
                                op0=ALU.is_lt, op1=ALU.mult, accum_out=under[:, k:k + 1]))
                            ch.join()
                            ch.step(nc.vector.max(top8[:, k, :], kept[:, k, :]))
                            ch.step(nc.vector.tensor_tensor(above[:, k:k + 1], total[:, slot:slot + 1],
                                                            under[:, k:k + 1], ALU.subtract))
                            ch.join()
                            ch.step(nc.vector.tensor_tensor_scan(cum8[:, k, :], ones8[:, :], top8[:, k, :],
                                                                 above[:, k:k + 1], ALU.mult, ALU.add))
                            ch.join()
                            ch.step(nc.vector.scalar_tensor_tensor(
                                out=reached8[:, k, 0:7], in0=cum8[:, k, 0:7], scalar=goal[:, slot:slot + 1],
                                in1=top8[:, k, 0:7], op0=ALU.is_ge, op1=ALU.mult))
                            ch.step(nc.vector.tensor_copy(reached8[:, k, 7:8], top8[:, k, 7:8]))
                            ch.join()
                            ch.step(nc.vector.reduce_max(edge[:, k:k + 1], reached8[:, k, :], AX))
                            ch.join()
                            ch.step(nc.vector.scalar_tensor_tensor(
                                out=kept[:, k, :], in0=e[:, slot, :], scalar=edge[:, k:k + 1], in1=e[:, slot, :],
                                op0=ALU.is_ge, op1=ALU.mult, accum_out=sum_ge[:, k:k + 1]))
                            ch.step(nc.vector.scalar_tensor_tensor(
                                out=cum8[:, k, :], in0=top8[:, k, :], scalar=edge[:, k:k + 1], in1=top8[:, k, :],
                                op0=ALU.is_gt, op1=ALU.mult, accum_out=sum_gt[:, k:k + 1]))

                    def weigh(half):
                        goals = goal[:, 2 * half:2 * half + 2]
                        ch.step(nc.vector.tensor_tensor(sum_gt[:, :], sum_gt[:, :], above[:, :], ALU.add))
                        ch.step(nc.vector.reciprocal(rcp_edge[:, :], edge[:, :]))
                        ch.step(nc.vector.scalar_tensor_tensor(out=hold[:, :], in0=goals, scalar=1.0 - SLACK,
                                                               in1=sum_ge[:, :], op0=ALU.mult, op1=ALU.is_gt))
                        ch.join()
                        ch.step(nc.vector.tensor_tensor(n_tied[:, :], sum_ge[:, :], sum_gt[:, :], ALU.subtract))
                        ch.step(nc.vector.tensor_tensor(n_kept[:, :], goals, sum_gt[:, :], ALU.subtract))
                        ch.join()
                        ch.step(nc.vector.tensor_tensor(n_tied[:, :], n_tied[:, :], rcp_edge[:, :], ALU.mult))
                        ch.step(nc.vector.tensor_tensor(n_kept[:, :], n_kept[:, :], rcp_edge[:, :], ALU.mult))
                        ch.join()
                        ch.step(nc.vector.tensor_scalar(n_tied[:, :], n_tied[:, :], ROUND, ROUND, ALU.add, ALU.subtract))
                        ch.step(nc.vector.tensor_scalar(n_kept[:, :], n_kept[:, :], 0.495, ROUND, ALU.add, ALU.add))
                        ch.join()
                        ch.step(nc.vector.tensor_scalar(n_tied[:, :], n_tied[:, :], 1.0, None, ALU.max))
                        ch.step(nc.vector.tensor_scalar(n_kept[:, :], n_kept[:, :], ROUND, 1.0, ALU.subtract, ALU.max))
                        ch.join()
                        ch.step(nc.vector.tensor_tensor(n_kept[:, :], n_kept[:, :], n_tied[:, :], ALU.min))
                        ch.step(nc.vector.reciprocal(rcp_tied[:, :], n_tied[:, :]))
                        ch.join()
                        ch.step(nc.vector.tensor_tensor(cut[:, :], n_tied[:, :], n_kept[:, :], ALU.subtract))
                        ch.join()
                        ch.step(nc.vector.tensor_scalar(n_kept[:, :], cut[:, :], 1.0, None, ALU.min))
                        ch.step(nc.vector.tensor_tensor(cut[:, :], cut[:, :], edge[:, :], ALU.mult))
                        ch.join()
                        ch.step(nc.vector.scalar_tensor_tensor(out=n_kept[:, :], in0=hold[:, :], scalar=16.0,
                                                               in1=n_kept[:, :], op0=ALU.mult, op1=ALU.max))
                        ch.step(nc.vector.tensor_tensor(kept_sum[:, :], sum_ge[:, :], cut[:, :], ALU.subtract))
                        ch.join()
                        ch.step(nc.vector.reduce_max(code32[:, 0:1], n_kept[:, :], AX))
                        ch.step(nc.vector.tensor_tensor(cut[:, :], cut[:, :], rcp_tied[:, :], ALU.mult))
                        ch.step(nc.vector.reciprocal(kept_sum[:, :], kept_sum[:, :]))
                        ch.join()
                        ch.step(nc.vector.transpose(code_t[:, :], code32[:, :]))
                        ch.step(nc.vector.tensor_scalar(a_rcp[:, 2 * half:2 * half + 2], kept_sum[:, :],
                                                        1.0 / (SE * SX), None, ALU.mult))
                        ch.join()
                        ch.step(nc.vector.reduce_max(code_4[:, 0:1], code_t[:, :], AX))
                        ch.join()
                        for r in range(1, 4):
                            ch.step(nc.vector.tensor_copy(code_4[0:1, r:r + 1], code_4[r * 32:r * 32 + 1, 0:1]))
                        ch.join()
                        ch.step(nc.vector.reduce_max(code_i[0:1, :], code_4[0:1, :], AX))
                        ch.restart()

                    def code():
                        return dve.value_load(code_i[0:1, 0:1], min_val=0, max_val=16)

                    def keep(q, half):
                        after(dve, y_ready, q * 2 - 2)
                        weigh(half)
                        with dve.While(lambda: code() >= 16):
                            for k in range(2):
                                slot_thr = thr[:, 2 * half + k:2 * half + k + 1]
                                ch.step(nc.vector.tensor_scalar(hit[:, k:k + 1], hold[:, k:k + 1], -1.0, 1.0,
                                                                ALU.mult, ALU.add))
                                ch.join()
                                ch.step(nc.vector.tensor_tensor(hit[:, k:k + 1], hit[:, k:k + 1], slot_thr,
                                                                ALU.mult))
                                ch.join()
                                ch.step(nc.vector.tensor_tensor(slot_thr, hit[:, k:k + 1], edge[:, k:k + 1],
                                                                ALU.max))
                                ch.join()
                            locate(half, (0, 1))
                            ch.join()
                            weigh(half)
                        with dve.If(code() >= 1):
                            for k in range(2):
                                slot = 2 * half + k
                                ch.step(nc.vector.tensor_scalar(e[:, slot, :], kept[:, k, :], edge[:, k:k + 1],
                                                                cut[:, k:k + 1], ALU.is_equal, ALU.mult))
                                ch.join()
                                ch.step(nc.vector.tensor_tensor(kept[:, k, :], kept[:, k, :], e[:, slot, :],
                                                                ALU.subtract))
                                ch.join()
                            ch.restart()
                        dve.sem_inc(kept_ready, 2)

                    for k in range(2):
                        maximum(k, k)
                    ch.restart()

                    def pair(q, half, before_last, last, this, after_this):
                        other = 1 - half
                        if this:
                            dve.wait_ge(exp_ready, q * 2 + 1)
                            tot = total[:, 2 * half:2 * half + 1]
                            ch.step(nc.vector.tensor_scalar(goal[:, 2 * half:2 * half + 1], tot, TOP_P, None, ALU.mult))
                            ch.step(nc.vector.tensor_scalar(thr[:, 2 * half:2 * half + 1], tot, lower_end * first_ratio, None, ALU.mult))
                            ch.join()
                        for h in range(halvings + 2):
                            if this:
                                if h < halvings:
                                    halve(2 * half, h)
                                elif h == halvings:
                                    locate(half, (0,))
                                else:
                                    dve.wait_ge(thr_final, q + 1)
                                    locate(half, (1,))
                                    ch.join()
                                    keep(q, half)
                            for what, k, *chunks in DVE_AFTER[p].get(h, ()):
                                if what == "a_low" and last:
                                    a_low(q * 2 - 2 + k, *chunks)
                                if what == "max" and after_this:
                                    maximum(q * 2 + 2 + k, 2 * other + k)
                                if what == "s_sum" and this:
                                    s_sum(q * 2 + k)
                                if what == "r_out" and this:
                                    r_out(q, k)
                                if what == "r_out_last" and last:
                                    r_out(q - 1, k)
                                if what == "y_low" and last:
                                    y_low(q * 2 - 2 + k, k)
                                if what == "y_sum" and last:
                                    y_sum(q, k, 2 * other + k)
                                if what == "normalise" and before_last:
                                    normalise(q, k)
                        ch.restart()
                    skewed(dve, pair)

        stage_norm()
        for p in range(2):
            stage_project(p)
            stage_multiply(p)


def kernel(x, adj, L0_gnn_W1, L0_gnn_W2, L0_gnn_W3, L0_gnn_U1_0, L0_gnn_U1_1, L0_gnn_U2_0, L0_gnn_U2_1,
           L0_gnn_gamma, L0_gnn_beta):
    import numpy as np
    import concourse.bacc as bacc
    from concourse.bass_utils import run_bass_kernel_spmd

    n = x.shape[0]
    adj_t = np.ascontiguousarray(np.asarray(adj).reshape(n // P, P, n // P, P).transpose(0, 3, 2, 1))
    given = {
        "x": x, "adj_t": adj_t.reshape(n // P, P, n), "w1_t": np.asarray(L0_gnn_W1).T, "w2": L0_gnn_W2,
        "w3": L0_gnn_W3, "u1_0": L0_gnn_U1_0, "u1_1": L0_gnn_U1_1, "u2_0": L0_gnn_U2_0, "u2_1": L0_gnn_U2_1,
        "gamma": L0_gnn_gamma, "beta": L0_gnn_beta,
    }
    nc = bacc.Bacc("TRN2", target_bir_lowering=False, num_devices=1)
    arrays, args = {}, []
    for name, a in given.items():
        arrays[name] = np.ascontiguousarray(a)
        args.append(nc.dram_tensor(name, arrays[name].shape, mybir.dt.from_np(arrays[name].dtype),
                                   kind="ExternalInput").ap())
    args.append(nc.dram_tensor("out", x.shape, F32, kind="ExternalOutput").ap())
    gnn_layer(nc, *args)
    return run_bass_kernel_spmd(nc, [arrays], core_ids=[0]).results[0]["out"]
```

```python
import concourse.bass as bass
from concourse import mybir
from contextlib import ExitStack

F32 = mybir.dt.float32
F16 = mybir.dt.float16
I32 = mybir.dt.int32
U8 = mybir.dt.uint8
ALU = mybir.AluOpType
ACT = mybir.ActivationFunctionType
AX = mybir.AxisListType.X

P = 128
TOP_P = 0.9
LN_EPS = 1e-5

SX = 64.0
SW = 64.0
SE = 1024.0
SQ = 32.0

HALVINGS = (7, 11)
EARLY = (0, 1)
ROUND = 12582912.0
SLACK = 1e-5


ACT_AFTER = (
    {0: (("a_high", 0, (0, 1)), ("a_high", 0, (2, 3))), 1: (("exp", 0),), 3: (("s_high", 1),),
     4: (("y", 0), ("a_high", 1, (0, 1))), 5: (("a_high", 1, (2, 3)),), 6: (("exp", 1),),
     7: (("y_high", 0), ("s_high", 0), ("y", 1), ("y_high", 1))},
    {3: (("a_high", 0, (0, 1)), ("a_high", 0, (2, 3))), 4: (("exp", 0), ("s_high", 1)),
     6: (("a_high", 1, (0, 1)),), 7: (("exp", 1), ("a_high", 1, (2, 3))), 8: (("early", 0),),
     9: (("s_high", 0),)})
DVE_AFTER = (
    {0: (("a_low", 0, (0, 1)),), 1: (("a_low", 0, (2, 3)), ("max", 0)), 2: (("s_sum", 0),),
     4: (("r_out_last", 1),), 6: (("a_low", 1, (0, 1)), ("max", 1)), 7: (("a_low", 1, (2, 3)), ("s_sum", 1)),
     8: (("y_low", 0), ("r_out", 0), ("y_low", 1))},
    {0: (("a_low", 0, (0, 1)),), 1: (("a_low", 0, (2, 3)), ("max", 0)), 3: (("normalise", 0), ("normalise", 1)),
     6: (("a_low", 1, (0, 1)), ("max", 1)), 7: (("a_low", 1, (2, 3)),), 8: (("y_sum", 0),), 10: (("r_out", 0),),
     12: (("y_sum", 1), ("r_out", 1))})
POOL_AFTER = (
    {3: (("s_low", 1, (0, 1)),), 4: (("s_low", 1, (2, 3)), ("start", 0)),
     6: (("start", 1), ("s_low", 0, (0, 1, 2, 3)))},
    {4: (("rstd", 0), ("rstd", 1), ("s_low", 1, (0, 1))), 5: (("scale", 0), ("s_low", 1, (2, 3))),
     6: (("shift", 0), ("start", 0)), 7: (("add", 0), ("scale", 1)), 8: (("early", 0), ("shift", 1)),
     9: (("add", 1), ("s_low", 0, (0, 1))), 10: (("start", 1), ("s_low", 0, (2, 3)))})


def bracket_steps(n_cols, halvings):
    span = (n_cols / (1.0 - TOP_P)) * 1.05
    ratio = [span ** (0.5 ** (k + 1)) for k in range(halvings)]
    steps = [(ratio[k + 1] - ratio[k + 1] / ratio[k], ratio[k + 1] / ratio[k]) for k in range(halvings - 1)]
    up = 1.0 + 2.0 ** -17
    return ratio[0], steps + [((ratio[-1] - 1.0) * up, up)]


class Chain:

    def __init__(self, eng, sem):
        self.eng, self.sem, self.n = eng, sem, 0

    def step(self, ins):
        ins.then_inc(self.sem, 1)
        self.n += 1

    def join(self):
        self.eng.wait_ge(self.sem, self.n)

    def restart(self):
        if self.n:
            self.join()
            self.eng.sem_clear(self.sem)
            self.n = 0


def gnn_layer(nc, x, adj_t, w1_t, w2, w3, u1_0, u1_1, u2_0, u2_1, gamma, beta, out):
    N, D = x.shape
    DA = w2.shape[0]
    NT, DT = N // P, D // P
    CH = 512
    SMALL_COLS = 160
    NC = N // CH
    NPAIR = NT // 2
    BLK = CH // P
    lower_end = (1.0 - TOP_P) / N * (1.0 - 2.0 ** -12)

    ctx = ExitStack()
    with ctx:
        def sb(name, shape, dt=F32):
            return ctx.enter_context(nc.sbuf_tensor(name, shape, dt))

        def ps(name, shape, dt=F32):
            return ctx.enter_context(nc.psum_tensor(name, shape, dt))

        def sem(name):
            return ctx.enter_context(nc.semaphore(name))

        def split(name, shape):
            return sb(name + "_hi", shape, F16), sb(name + "_lo", shape, F16)

        h_dram = nc.dram_tensor("h_scratch", [NT, P, D], F32, kind="Internal")
        base_dram = [nc.dram_tensor(f"base_scratch{p}", [NT, P, D], F32, kind="Internal") for p in range(2)]
        v_dram = nc.dram_tensor("v_scratch", [NT, P, D], F32, kind="Internal")

        mov_hi, mov_lo = split("mov", [P, NT, D])
        feat_hi, feat_lo = split("feat_t", [P, DT, N])
        vec_hi, vec_lo = split("vec", [P, NT, D])
        e = sb("e", [P, 4, N])
        kept = sb("kept", [P, 2, N])
        scrap = sb("scrap", [P, 3, N], U8)
        at_hi, at_lo = split("a_t", [P, NT, P])
        s_in = sb("s_in", [P, N])
        s_hi, s_lo = split("s", [P, 2, N])
        query = sb("query", [P, N], F16)
        key_hi, key_lo = split("key", [P, N])
        row_in = sb("row_in", [P, 2, D])
        y_row = sb("y_row", [P, 2, D])
        ident = sb("ident", [P, P])
        ident_h = sb("ident_h", [P, P], F16)
        ones_h = sb("ones_h", [P, 1], F16)
        small = sb("small", [P, SMALL_COLS])
        taken = [0]

        def columns(n):
            taken[0] += n
            return small[:, taken[0] - n:taken[0]]

        stats = sb("stats", [P, 2, 6])
        mean_var = sb("mean_var", [P, 2, 2])
        rstd = columns(2)
        shift = columns(2)
        half_col = columns(1)
        goal_col = columns(1)
        minus_col = columns(1)
        row_max = columns(4)
        neg_max = columns(4)
        total = columns(4)
        s_rcp = columns(NT)
        a_rcp = columns(4)
        goal = columns(4)
        thr = columns(4)
        above = columns(2)
        hit = columns(2)
        under = columns(2)
        top8 = sb("top8", [P, 2, 8])
        cum8 = sb("cum8", [P, 2, 8])
        reached8 = sb("reached8", [P, 2, 8])
        edge = columns(2)
        sum_ge = columns(2)
        sum_gt = columns(2)
        rcp_edge = columns(2)
        n_tied = columns(2)
        n_kept = columns(2)
        cut = columns(2)
        kept_sum = columns(2)
        rcp_tied = columns(2)
        ones8 = columns(8)
        n_col = columns(1)
        neg_thr = columns(2)
        next_thr = columns(2)
        excess = columns(2)
        signs = columns(2)
        reach = columns(2)
        hold = columns(2)
        code32 = columns(32)
        code_t = columns(32)
        code_4 = columns(4)
        assert taken[0] <= SMALL_COLS
        code_i = sb("code_i", [P, 1], I32)

        ua = [s[:, 0, :].rearrange("p (t n) -> p t n", t=DT) for s in (s_hi, s_lo)]
        ub = [s[:, 1, :].rearrange("p (t n) -> p t n", t=DT) for s in (s_hi, s_lo)]
        u_raw = [e[:, k, :].rearrange("p (t n) -> p t n", t=DT) for k in range(2)]
        qk_w = sb("qk_w", [P, 2, 2, DT, P], F16)
        w_hi, w_lo = qk_w[:, 0], qk_w[:, 1]
        last_rows = qk_w[:, :].rearrange("p a b c d -> p (a b c d)").bitcast(F32)
        gamma_b, beta_b = last_rows[:, 0:D], last_rows[:, D:2 * D]
        wk_raw = e[:, 2, 0:DT * P].rearrange("p (t n) -> p t n", t=DT)
        w1_raw = e[0:DA, 2, DT * P:DT * P + D]
        w2_raw = e[0:DA, 2, DT * P + D:DT * P + D + P]

        r_rows = [f[:, :, :].rearrange("p d n -> p (d n)").bitcast(F32).rearrange("p (q n) -> p q n", n=D)
                  for f in (feat_hi, feat_lo)]

        logits = ps("logits", [P, N])
        turn = ps("turn", [P, 2, CH])
        acc_a = ps("acc_a", [P, CH])
        acc_r = ps("acc_r", [P, CH])

        def split_hi(dst, src, scale):
            return nc.scalar.activation(dst, src, ACT.Copy, scale=scale)

        def split_lo(dst, src, hi, scale):
            return nc.vector.scalar_tensor_tensor(out=dst, in0=src, scalar=scale, in1=hi,
                                                  op0=ALU.mult, op1=ALU.subtract)

        def product3(psum, left, right, count, opens=True):
            for k in range(count):
                l_hi, l_lo, r_hi, r_lo = left(0, k), left(1, k), right(0, k), right(1, k)
                nc.tensor.matmul(psum, l_hi, r_hi, start=(opens and k == 0), stop=False)
                nc.tensor.matmul(psum, l_hi, r_lo, start=False, stop=False)
                last = nc.tensor.matmul(psum, l_lo, r_hi, start=False,
                                        stop=(k == count - 1))
            return last

        def cols(t):
            return bass.ds(t * P, P)

        def plane(tile3, t):
            return tile3[:, bass.ds(t, 1), :].rearrange("p a d -> p (a d)")

        def dram_rows(tensor, t):
            return tensor[bass.ds(t, 1), :, :].rearrange("a p d -> p (a d)")

        def after(eng, semaphore, value):
            if not isinstance(value, int) or value > 0:
                eng.wait_ge(semaphore, value)

        def by_pairs(eng, body):
            body(0)
            with eng.Fori(1, NPAIR) as q:
                body(q)

        base_row = kept[:, 0, 0:2 * D].rearrange("p (k n) -> p k n", k=2)

        def stage_norm():
            const_ready = sem("const_ready")
            gp_step = sem("gp_step")
            w_loaded = sem("w_loaded")
            u_loaded = sem("u_loaded0")
            u_hi_ready = sem("u_hi_ready0")
            u_lo_ready = sem("u_lo_ready0")
            x_loaded = [sem(f"x_loaded{k}") for k in range(2)]
            var_ready = sem("var_ready")
            rstd_ready = sem("rstd_ready")
            shift_ready = sem("shift_ready")
            h_ready = sem("h_ready")
            h_hi_ready = sem("h_hi_ready")
            h_lo_ready = sem("h_lo_ready")
            h_turned = sem("h_turned")
            ft_hi_ready = sem("ft_hi_ready")
            ft_lo_ready = sem("ft_lo_ready")
            h_stored = [sem(f"h_stored{k}") for k in range(2)]
            w12_ready = sem("w12_ready")
            w_hi_ready = sem("w_hi_ready")
            dve_step = sem("norm_dve_step")
            prod_done = sem("prod_done0")
            vec_hi_ready = sem("vec_hi_ready")
            vec_lo_ready = sem("vec_lo_ready")
            base_ready = sem("base_ready0")
            base_stored = [sem(f"base_stored0_{k}") for k in range(2)]

            def by_pairs(eng, body):
                body(0, True, False)
                body(1, True, True)
                with eng.Fori(2, NPAIR) as q:
                    body(q, True, True)
                body(NPAIR, False, True)

            with nc.Block() as block:
                @block.sync
                def _(sp):
                    w3_rows = w3.rearrange("(t p) n -> p t n", p=P)

                    def load_x(t, k):
                        after(sp, h_ready, t - 1)
                        sp.dma_start(row_in[:, k, :], x[cols(t), :]).then_inc(x_loaded[k], 16)

                    sp.dma_start(w1_raw, w1_t).then_inc(w_loaded, 16)
                    sp.dma_start(w2_raw[:, 0:DA], w2).then_inc(w_loaded, 16)
                    sp.dma_start(w2_raw[:, DA:P], w2).then_inc(w_loaded, 16)
                    for k in range(2):
                        load_x(k, k)
                    sp.dma_start(wk_raw[:, :, 0:DA], w3_rows).then_inc(w_loaded, 16)
                    sp.dma_start(wk_raw[:, :, DA:P], w3_rows).then_inc(w_loaded, 16)
                    for k, w in enumerate((u1_1, u1_0)):
                        sp.dma_start(u_raw[k], w.rearrange("(t p) n -> p t n", p=P)).then_inc(u_loaded, 16)

                    def pair(q, this, last):
                        for k in range(2):
                            if this:
                                t = q * 2 + k
                                if last:
                                    load_x(t, k)
                        for k in range(2):
                            if this:
                                t = q * 2 + k
                                sp.wait_ge(h_ready, t + 1)
                                sp.dma_start(dram_rows(h_dram, t), y_row[:, k, :]).then_inc(h_stored[k], 16)
                    by_pairs(sp, pair)
                    for k in range(2):
                        sp.wait_ge(h_stored[k], 16 * NPAIR)

                @block.gpsimd
                def _(gp):
                    nc.gpsimd.memset(ident[:, :], 0.0).then_inc(gp_step, 1)
                    nc.gpsimd.memset(half_col[:, :], -0.5).then_inc(gp_step, 1)
                    gp.wait_ge(gp_step, 2)
                    nc.gpsimd.affine_select(out=ident[:, :], in_=ident[:, :], compare_op=ALU.not_equal, fill=1.0,
                                            base=0, pattern=[[-1, P]], channel_multiplier=1).then_inc(gp_step, 1)
                    gp.wait_ge(gp_step, 3)
                    nc.gpsimd.tensor_copy(ident_h[:, :], ident[:, :]).then_inc(const_ready, 1)
                    nc.gpsimd.memset(ones_h[:, :], 1.0)
                    nc.gpsimd.memset(ones8[:, :], 1.0)
                    nc.gpsimd.memset(minus_col[:, :], -1.0)
                    nc.gpsimd.memset(goal_col[:, :], TOP_P)
                    nc.gpsimd.memset(n_col[:, :], float(N))
                    nc.gpsimd.memset(code32[:, :], 0.0)

                    def pair(q, this, last):
                        for k in range(2):
                            if this:
                                t = q * 2 + k
                                gp.wait_ge(var_ready, t + 1)
                                after(gp, h_ready, t - 1)
                                nc.gpsimd.tensor_tensor(rstd[:, k:k + 1], mean_var[:, k, 1:2], half_col[:, :],
                                                        ALU.pow).then_inc(rstd_ready, 1)
                        for k in range(2):
                            if last:
                                t = q * 2 - 2 + k
                                gp.wait_ge(base_ready, t + 1)
                                gp.dma_start(dram_rows(base_dram[0], t), base_row[:, k, :]
                                             ).then_inc(base_stored[k], 16)
                    by_pairs(gp, pair)
                    for k in range(2):
                        gp.wait_ge(base_stored[k], 16 * NPAIR)

                @block.vector
                def _(dve):
                    ch = Chain(dve, dve_step)
                    nc.vector.memset(key_lo[:, :], 0.0)

                    def moments(q):
                        for k in range(2):
                            t = q * 2 + k
                            after(dve, rstd_ready, t - 1)
                            after(dve, shift_ready, t - 1)
                            dve.wait_ge(x_loaded[k], (q + 1) * 16)
                            ch.step(nc.vector.bn_stats(stats[:, k, :], row_in[:, k, :]))
                            ch.join()
                            ch.step(nc.vector.bn_aggr(mean_var[:, k, :], stats[:, k, :]))
                            ch.join()
                            nc.vector.tensor_scalar(mean_var[:, k, 1:2], mean_var[:, k, 1:2], LN_EPS, None,
                                                    ALU.add).then_inc(var_ready, 1)
                        for k in range(2):
                            t = q * 2 + k
                            dve.wait_ge(rstd_ready, t + 1)
                            after(dve, h_ready, t - 1)
                            nc.vector.scalar_tensor_tensor(out=shift[:, k:k + 1], in0=mean_var[:, k, 0:1], scalar=-1.0,
                                                           in1=rstd[:, k:k + 1], op0=ALU.mult,
                                                           op1=ALU.mult).then_inc(shift_ready, 1)

                    def h_low(t, k):
                        dve.wait_ge(h_hi_ready, t + 1)
                        split_lo(plane(mov_lo, t), y_row[:, k, :], plane(mov_hi, t), SX).then_inc(h_lo_ready, 1)
                        dve.wait_ge(ft_hi_ready, t + 1)
                        split_lo(feat_lo[:, :, cols(t)], turn[:, k, :].rearrange("p (d n) -> p d n", d=DT),
                                 feat_hi[:, :, cols(t)], SX).then_inc(ft_lo_ready, 1)

                    def products_out(t, k, stored):
                        dve.wait_ge(vec_hi_ready, t + 1)
                        split_lo(plane(vec_lo, t), logits[:, k * CH:(k + 1) * CH], plane(vec_hi, t),
                                 1.0 / SW).then_inc(vec_lo_ready, 1)
                        dve.wait_ge(prod_done, t * 2 + 2)
                        after(dve, base_stored[k], stored * 16)
                        nc.vector.tensor_scalar(base_row[:, k, :], logits[:, (2 + k) * CH:(3 + k) * CH],
                                                1.0 / (SX * SW), None, ALU.mult).then_inc(base_ready, 1)

                    def pair(q, this, last):
                        if this:
                            moments(q)
                        if not last:
                            dve.wait_ge(w_hi_ready, 1)
                            split_lo(w_lo[:, 0].rearrange("p t n -> p (t n)"), acc_a[:, :],
                                     w_hi[:, 0].rearrange("p t n -> p (t n)"), SW)
                            dve.wait_ge(w_hi_ready, 2)
                            split_lo(w_lo[:, 1], wk_raw, w_hi[:, 1], SW)
                        if last:
                            products_out(q * 2 - 2, 0, q - 1)
                        if this:
                            for k in range(2):
                                h_low(q * 2 + k, k)
                            ch.restart()
                        if not last:
                            for k, u in enumerate((ua, ub)):
                                dve.wait_ge(u_hi_ready, k + 1)
                                split_lo(u[1], u_raw[k], u[0], SW).then_inc(u_lo_ready, 1)
                        if last:
                            products_out(q * 2 - 1, 1, q - 1)
                    by_pairs(dve, pair)

                @block.scalar
                def _(act):
                    def h_rows(q):
                        for k in range(2):
                            t = q * 2 + k
                            act.wait_ge(shift_ready, t + 1)
                            after(act, h_stored[k], q * 16)
                            after(act, h_lo_ready, t - 1)
                            after(act, h_turned, t - 1)
                            nc.scalar.activation(y_row[:, k, :], row_in[:, k, :], ACT.Relu, bias=shift[:, k:k + 1],
                                                 scale=rstd[:, k:k + 1]).then_inc(h_ready, 1)

                    def h_high(t, k):
                        act.wait_ge(h_ready, t + 1)
                        split_hi(plane(mov_hi, t), y_row[:, k, :], SX).then_inc(h_hi_ready, 1)
                        act.wait_ge(h_turned, t + 1)
                        split_hi(feat_hi[:, :, cols(t)], turn[:, k, :].rearrange("p (d n) -> p d n", d=DT),
                                 SX).then_inc(ft_hi_ready, 1)

                    def vec_high(t, k):
                        act.wait_ge(prod_done, t * 2 + 1)
                        split_hi(plane(vec_hi, t), logits[:, k * CH:(k + 1) * CH], 1.0 / SW).then_inc(vec_hi_ready, 1)

                    def pair(q, this, last):
                        if not last:
                            act.wait_ge(w12_ready, 1)
                            split_hi(w_hi[:, 0].rearrange("p t n -> p (t n)"), acc_a[:, :], SW).then_inc(w_hi_ready, 1)
                        if this:
                            h_rows(q)
                        if not last:
                            act.wait_ge(w_loaded, 16 * 5)
                            split_hi(w_hi[:, 1], wk_raw, SW).then_inc(w_hi_ready, 1)
                        if last:
                            vec_high(q * 2 - 2, 0)
                        if this:
                            for k in range(2):
                                h_high(q * 2 + k, k)
                        if not last:
                            act.wait_ge(u_loaded, 32)
                            for k, u in enumerate((ua, ub)):
                                split_hi(u[0], u_raw[k], SW).then_inc(u_hi_ready, 1)
                        if last:
                            vec_high(q * 2 - 1, 1)
                    by_pairs(act, pair)

                @block.tensor
                def _(pe):
                    pe.wait_ge(w_loaded, 16 * 5)
                    for d in range(DT):
                        last_12 = nc.tensor.matmul(acc_a[:, d * P:(d + 1) * P], w1_raw[:, d * P:(d + 1) * P], w2_raw,
                                                   start=True, stop=True)
                    last_12.then_inc(w12_ready, 1)
                    pe.wait_ge(const_ready, 1)

                    def products(t, k):
                        pe.wait_ge(ft_lo_ready, t + 1)
                        for w, u in enumerate((ua, ub)):
                            after(pe, (vec_lo_ready, base_ready)[w], t - 1)
                            bank = 2 * w + k
                            product3(logits[:, bank * CH:(bank + 1) * CH],
                                     lambda part, d: (feat_hi, feat_lo)[part][:, d, cols(t)],
                                     lambda part, d: u[part][:, d, :], DT).then_inc(prod_done, 1)

                    def pair(q, this, last):
                        if last:
                            products(q * 2 - 2, 0)
                        if this:
                            for k in range(2):
                                t = q * 2 + k
                                pe.wait_ge(h_ready, t + 1)
                                after(pe, ft_lo_ready, t - 1)
                                for d in range(DT):
                                    done = nc.tensor.transpose(turn[:, k, d * P:(d + 1) * P],
                                                               y_row[:, k, d * P:(d + 1) * P], ident[:, :])
                                done.then_inc(h_turned, 1)
                        if not last:
                            pe.wait_ge(u_lo_ready, 2)
                        if last:
                            products(q * 2 - 1, 1)
                    by_pairs(pe, pair)

        def stage_project(p):
            qk_done = sem(f"qk_done{p}")
            qk_hi_ready = sem(f"qk_hi_ready{p}")
            qk_lo_ready = sem(f"qk_lo_ready{p}")
            if p == 1:
                u_loaded = sem("u_loaded")
                u_hi_ready = sem("u_hi_ready")
                u_lo_ready = sem("u_lo_ready")
                prod_done = sem("prod_done")
                mov_hi_ready = sem("mov_hi_ready")
                mov_lo_ready = sem("mov_lo_ready")
                base_ready = sem("base_ready")
                base_stored = [sem(f"base_stored{k}") for k in range(2)]
                h_loaded = [sem(f"h_loaded{k}") for k in range(2)]
                v_loaded = [sem(f"v_loaded{k}") for k in range(2)]
                v_hi_ready = sem("v_hi_ready")
                v_lo_ready = sem("v_lo_ready")

            with nc.Block() as block:
                if p == 1:
                    @block.sync
                    def _(sp):
                        for k, w in enumerate((u2_1, u2_0)):
                            sp.dma_start(u_raw[k], w.rearrange("(t p) n -> p t n", p=P)).then_inc(u_loaded, 16)

                        def pair(q):
                            for k in range(2):
                                t = q * 2 + k
                                after(sp, base_stored[k], q * 16)
                                sp.dma_start(row_in[:, k, :], dram_rows(h_dram, t)).then_inc(h_loaded[k], 16)
                                after(sp, v_lo_ready, t - 1)
                                sp.dma_start(y_row[:, k, :], dram_rows(v_dram, t)).then_inc(v_loaded[k], 16)
                            for k in range(2):
                                t = q * 2 + k
                                sp.wait_ge(base_ready, t + 1)
                                sp.dma_start(dram_rows(base_dram[1], t), row_in[:, k, :]).then_inc(base_stored[k], 16)
                        by_pairs(sp, pair)
                        for k in range(2):
                            sp.wait_ge(base_stored[k], 16 * NPAIR)

                @block.tensor
                def _(pe):
                    for c in range(NC):
                        for w in range(2):
                            after(pe, qk_lo_ready, 2 * c + w - 1)
                            product3(turn[:, w, :], lambda part, d: (w_hi, w_lo)[part][:, w, d, :],
                                     lambda part, d: (feat_hi, feat_lo)[part][:, d, c * CH:(c + 1) * CH],
                                     DT).then_inc(qk_done, 1)
                    if p == 0:
                        return
                    pe.wait_ge(u_lo_ready, 2)

                    def pair(q):
                        for k in range(2):
                            t = q * 2 + k
                            for w, u in enumerate((ua, ub)):
                                after(pe, (mov_lo_ready, base_ready)[w], t - 1)
                                bank = 2 * w + k
                                product3(logits[:, bank * CH:(bank + 1) * CH],
                                         lambda part, d: (feat_hi, feat_lo)[part][:, d, cols(t)],
                                         lambda part, d: u[part][:, d, :], DT).then_inc(prod_done, 1)
                    by_pairs(pe, pair)

                @block.scalar
                def _(act):
                    for c in range(NC):
                        if p == 1 and c >= NC - 2:
                            k = c - (NC - 2)
                            act.wait_ge(u_loaded, 32)
                            split_hi((ua, ub)[k][0], u_raw[k], SW).then_inc(u_hi_ready, 1)
                        for w in range(2):
                            act.wait_ge(qk_done, 2 * c + w + 1)
                            split_hi((query, key_hi)[w][:, c * CH:(c + 1) * CH], turn[:, w, :],
                                     SQ / (SX * SW)).then_inc(qk_hi_ready, 1)
                    if p == 0:
                        return

                    def pair(q):
                        for k in range(2):
                            t = q * 2 + k
                            act.wait_ge(prod_done, t * 2 + 1)
                            split_hi(plane(mov_hi, t), logits[:, k * CH:(k + 1) * CH],
                                     1.0 / SW).then_inc(mov_hi_ready, 1)
                            act.wait_ge(v_loaded[k], (q + 1) * 16)
                            split_hi(plane(vec_hi, t), y_row[:, k, :], SX).then_inc(v_hi_ready, 1)
                    by_pairs(act, pair)

                @block.vector
                def _(dve):
                    for c in range(NC):
                        if p == 1 and c >= NC - 2:
                            k = c - (NC - 2)
                            dve.wait_ge(u_hi_ready, k + 1)
                            split_lo((ua, ub)[k][1], u_raw[k], (ua, ub)[k][0], SW).then_inc(u_lo_ready, 1)
                        for w in range(2):
                            dve.wait_ge(qk_hi_ready, 2 * c + w + 1)
                            lo, hi = ((DA, P), (0, DA))[w]
                            span = slice(c * CH, (c + 1) * CH)
                            split_lo((query, key_lo)[w][lo:hi, span], turn[lo:hi, w, :],
                                     (query, key_hi)[w][lo:hi, span], SQ / (SX * SW)).then_inc(qk_lo_ready, 1)
                    if p == 0:
                        return

                    def pair(q):
                        for k in range(2):
                            t = q * 2 + k
                            dve.wait_ge(mov_hi_ready, t + 1)
                            split_lo(plane(mov_lo, t), logits[:, k * CH:(k + 1) * CH], plane(mov_hi, t),
                                     1.0 / SW).then_inc(mov_lo_ready, 1)
                            dve.wait_ge(prod_done, t * 2 + 2)
                            dve.wait_ge(h_loaded[k], (q + 1) * 16)
                            nc.vector.scalar_tensor_tensor(
                                out=row_in[:, k, :], in0=logits[:, (2 + k) * CH:(3 + k) * CH], scalar=1.0 / (SX * SW),
                                in1=row_in[:, k, :], op0=ALU.mult, op1=ALU.add).then_inc(base_ready, 1)
                            dve.wait_ge(v_hi_ready, t + 1)
                            split_lo(plane(vec_lo, t), y_row[:, k, :], plane(vec_hi, t),
                                     SX).then_inc(v_lo_ready, 1)
                    by_pairs(dve, pair)

        def stage_multiply(p):
            final = p == 1
            halvings = HALVINGS[p]
            by_act = (EARLY[p], halvings)
            first_ratio, steps = bracket_steps(N, halvings)
            s_loaded = sem(f"s_loaded{p}")
            s_hi_ready = sem(f"s_hi_ready{p}")
            s_lo_ready = sem(f"s_lo_ready{p}")
            base_loaded = [sem(f"base_loaded{p}_{k}") for k in range(2)]
            logits_done = sem(f"logits_done{p}")
            max_ready = sem(f"max_ready{p}")
            exp_ready = sem(f"exp_ready{p}")
            kept_ready = sem(f"kept_ready{p}")
            a_turned = sem(f"a_turned{p}")
            at_hi_ready = sem(f"at_hi_ready{p}")
            at_lo_ready = sem(f"at_lo_ready{p}")
            s_sum_done = sem(f"s_sum_done{p}")
            s_rcp_ready = sem(f"s_rcp_ready{p}")
            r_done = sem(f"r_done{p}")
            r_read = sem(f"r_read{p}")
            a_done = sem(f"a_done{p}")
            y_ready = sem(f"y_ready{p}")
            search_step = sem(f"search_step{p}")
            thr_set = [sem(f"thr_set{p}_{k}") for k in range(2)]
            sums_ready = [sem(f"sums_ready{p}_{k}") for k in range(2)]
            thr_final = [sem(f"thr_final{p}_{k}") for k in range(2)]
            update_step = sem(f"update_step{p}")
            if final:
                last_loaded = sem("last_loaded")
                x_loaded = [sem(f"last_x_loaded{k}") for k in range(2)]
                var_ready = sem("last_var_ready")
                rstd_ready = sem("last_rstd_ready")
                normed = sem("normed")
                out_stored = [sem(f"out_stored{k}") for k in range(2)]
            else:
                y_turned = sem("y_turned")
                y_hi_ready = sem("y_hi_ready")
                y_lo_ready = sem("y_lo_ready")
                v_stored = [sem(f"v_stored{k}") for k in range(2)]

            def skewed(eng, body):
                body(0, 0, False, False, True, True)
                body(1, 1, False, True, True, True)
                with eng.Fori(1, NPAIR // 2 - 1) as i:
                    body(i * 2, 0, True, True, True, True)
                    body(i * 2 + 1, 1, True, True, True, True)
                body(NPAIR - 2, 0, True, True, True, True)
                body(NPAIR - 1, 1, True, True, True, False)
                body(NPAIR, 0, True, True, False, False)
                if final:
                    body(NPAIR + 1, 1, True, False, False, False)

            with nc.Block() as block:
                @block.sync
                def _(sp):
                    def load_s(t):
                        after(sp, s_lo_ready, t)
                        sp.dma_start(s_in[:, :], adj_t[bass.ds(t, 1), :, :].rearrange("a p n -> p (a n)")
                                     ).then_inc(s_loaded, 16)

                    def load_base(t, k):
                        sp.dma_start(row_in[:, k, :], dram_rows(base_dram[p], t)).then_inc(base_loaded[k], 16)

                    def row_used(q, k, more):
                        sp.wait_ge(r_read, q * 2 + k + 1)
                        if not final:
                            sp.dma_start(dram_rows(v_dram, q * 2 + k), row_in[:, k, :]).then_inc(v_stored[k], 16)
                            sp.wait_ge(v_stored[k], (q + 1) * 16)
                        if more:
                            load_base(q * 2 + 2 + k, k)

                    load_s(0)
                    for k in range(2):
                        load_base(k, k)
                    if final:
                        for dst, row in ((gamma_b, gamma), (beta_b, beta)):
                            sp.dma_start(dst, row.rearrange("(a d) -> a d", a=1).to_broadcast([P, D])
                                         ).then_inc(last_loaded, 16)

                    def pair(q, half, before_last, last, this, after_this):
                        if this:
                            load_s(q * 2 + 1)
                        if last:
                            row_used(q - 1, 1, this)
                        if after_this:
                            load_s(q * 2 + 2)
                        if this:
                            row_used(q, 0, after_this)
                    skewed(sp, pair)
                    if final:
                        sp.wait_ge(last_loaded, 32)
                    else:
                        for k in range(2):
                            sp.wait_ge(v_stored[k], 16 * NPAIR)

                @block.gpsimd
                def _(gp):
                    if final:
                        gp.wait_ge(last_loaded, 32)

                    ch = Chain(gp, update_step)

                    def s_low(t, slot, chunks):
                        gp.wait_ge(s_hi_ready, t + 1)
                        for c in chunks:
                            span = slice(c * CH, (c + 1) * CH)
                            ins = nc.gpsimd.tensor_tensor(s_lo[:, slot, span], s_in[:, span], s_hi[:, slot, span],
                                                          ALU.subtract)
                            if c == NC - 1:
                                ins.then_inc(s_lo_ready, 1)


                    def start(q, half, k):
                        slot = 2 * half + k
                        tot = total[:, slot:slot + 1]
                        gp.wait_ge(exp_ready, q * 2 + k + 1)
                        ch.step(nc.gpsimd.tensor_tensor(goal[:, slot:slot + 1], tot, goal_col[:, :], ALU.mult))
                        ch.step(nc.gpsimd.tensor_scalar(neg_thr[:, k:k + 1], tot, -lower_end * first_ratio, None,
                                                        ALU.mult))
                        ch.join()
                        if by_act[k]:
                            gp.sem_inc(thr_set[k], 1)
                        else:
                            hand_over(slot, k)

                    def hand_over(slot, k):
                        ch.step(nc.gpsimd.tensor_tensor(thr[:, slot:slot + 1], neg_thr[:, k:k + 1], minus_col[:, :],
                                                        ALU.mult))
                        ch.join()
                        gp.sem_inc(thr_final[k], 1)

                    def update(q, half, k, h):
                        gain, miss = steps[h]
                        slot = 2 * half + k
                        neg, following, sum_k = neg_thr[:, k:k + 1], next_thr[:, k:k + 1], reach[:, k:k + 1]
                        ch.step(nc.gpsimd.tensor_scalar(following, neg, gain, None, ALU.mult))
                        gp.wait_ge(sums_ready[k], q * (2 * by_act[k]) + 2 * h + 2)
                        ch.step(nc.gpsimd.tensor_tensor(sum_k, signs[:, k:k + 1], n_col[:, :], ALU.add))
                        ch.join()
                        ch.step(nc.gpsimd.tensor_scalar(sum_k, sum_k, -0.5, neg, ALU.mult, ALU.mult))
                        ch.join()
                        ch.step(nc.gpsimd.tensor_scalar(sum_k, sum_k, excess[:, k:k + 1], goal[:, slot:slot + 1],
                                                        ALU.add, ALU.is_ge))
                        ch.join()
                        ch.step(nc.gpsimd.tensor_scalar(neg, sum_k, miss / gain, following, ALU.add, ALU.mult))
                        ch.join()
                        if h < by_act[k] - 1:
                            gp.sem_inc(thr_set[k], 1)
                        else:
                            hand_over(slot, k)

                    def finish_row(q, k, part):
                        t = q * 2 - 4 + k
                        y, r_part = y_row[:, k, :], plane(r_rows[k], q - 2)
                        if part == "rstd":
                            gp.wait_ge(var_ready, t + 1)
                            ch.step(nc.gpsimd.tensor_tensor(rstd[:, k:k + 1], mean_var[:, k, 1:2], half_col[:, :],
                                                            ALU.pow))
                            ch.join()
                            gp.sem_inc(rstd_ready, 1)
                            gp.dma_start(r_part, x[cols(t), :]).then_inc(x_loaded[k], 16)
                        if part == "scale":
                            gp.wait_ge(normed, t + 1)
                            ch.step(nc.gpsimd.tensor_tensor(y, y, gamma_b, ALU.mult))
                            ch.join()
                        if part == "shift":
                            gp.wait_ge(x_loaded[k], (q - 1) * 16)
                            ch.step(nc.gpsimd.tensor_tensor(y, y, beta_b, ALU.add))
                            ch.join()
                        if part == "add":
                            ch.step(nc.gpsimd.tensor_tensor(y, y, r_part, ALU.add))
                            ch.join()
                            gp.dma_start(out[cols(t), :], y).then_inc(out_stored[k], 16)

                    start(0, 0, 0)
                    for h in range(by_act[0]):
                        update(0, 0, 0, h)
                    start(0, 0, 1)
                    s_low(0, 0, range(NC))

                    def pair(q, half, before_last, last, this, after_this):
                        for h in range(halvings):
                            if this:
                                update(q, half, 1, h)
                            for what, k, *chunks in POOL_AFTER[p].get(h, ()):
                                if what == "s_low":
                                    if (after_this, this)[k]:
                                        s_low(q * 2 + 2 - k, k, *chunks)
                                elif what == "start":
                                    if after_this:
                                        start(q + 1, 1 - half, k)
                                elif what == "early":
                                    if after_this:
                                        update(q + 1, 1 - half, 0, k)
                                elif before_last:
                                    finish_row(q, k, what)
                        ch.restart()
                    skewed(gp, pair)
                    if final:
                        for k in range(2):
                            gp.wait_ge(out_stored[k], 16 * NPAIR)

                @block.scalar
                def _(act):
                    def s_high(t, slot):
                        act.wait_ge(s_loaded, t * 16 + 16)
                        after(act, r_done, t - 1)
                        split_hi(s_hi[:, slot, :], s_in[:, :], 1.0).then_inc(s_hi_ready, 1)

                    def exponential(t, slot):
                        act.wait_ge(max_ready, t + 1)
                        after(act, kept_ready, t - 3)
                        nc.scalar.activation(e[:, slot, :], logits[:, :], ACT.Exp, bias=neg_max[:, slot:slot + 1],
                                             scale=1.0 / (SQ * SQ), accum_out=total[:, slot:slot + 1]
                                             ).then_inc(exp_ready, 1)

                    def evaluate(q, half, k, h):
                        slot = 2 * half + k
                        act.wait_ge(thr_set[k], q * by_act[k] + h + 1)
                        nc.scalar.activation(scrap[:, 1, :], e[:, slot, :], ACT.Relu, bias=neg_thr[:, k:k + 1],
                                             accum_out=excess[:, k:k + 1]).then_inc(sums_ready[k], 1)
                        nc.scalar.activation(scrap[:, 2, :], e[:, slot, :], ACT.Sign, bias=neg_thr[:, k:k + 1],
                                             accum_out=signs[:, k:k + 1]).then_inc(sums_ready[k], 1)

                    def a_high(t, chunks):
                        after(act, a_done, t)
                        for c in chunks:
                            act.wait_ge(a_turned, t * BLK + c + 1)
                            split_hi(at_hi[:, c * BLK:(c + 1) * BLK, :],
                                     turn[:, c % 2, :].rearrange("p (b n) -> p b n", b=BLK), SE
                                     ).then_inc(at_hi_ready, 1)

                    def y_scaled(t, k, slot):
                        act.wait_ge(a_done, t + 1)
                        after(act, y_turned, t - 1)
                        nc.scalar.activation(y_row[:, k, :], acc_a[:, :], ACT.Copy,
                                             scale=a_rcp[:, slot:slot + 1]).then_inc(y_ready, 1)

                    def y_high(t, k):
                        act.wait_ge(y_turned, t + 1)
                        split_hi(feat_hi[:, :, cols(t)], turn[:, k, :].rearrange("p (d n) -> p d n", d=DT),
                                 SX).then_inc(y_hi_ready, 1)

                    for k in range(2):
                        exponential(k, k)
                    for h in range(by_act[0]):
                        evaluate(0, 0, 0, h)
                        act.wait_ge(sums_ready[0], 2 * h + 2)
                    s_high(0, 0)

                    def pair(q, half, before_last, last, this, after_this):
                        other = 1 - half
                        for h in range(halvings + 1):
                            if this and h < halvings:
                                evaluate(q, half, 1, h)
                            for what, k, *chunks in ACT_AFTER[p].get(h, ()):
                                if what == "a_high" and last:
                                    a_high(q * 2 - 2 + k, *chunks)
                                if what == "early" and after_this:
                                    act.wait_ge(sums_ready[1], q * (2 * halvings) + 2 * h + 2)
                                    evaluate(q + 1, other, 0, k)
                                    act.wait_ge(sums_ready[0], q * (2 * by_act[0]) + 2 * by_act[0] + 2 * k + 2)
                                if what == "exp" and after_this:
                                    exponential(q * 2 + 2 + k, 2 * other + k)
                                if what == "s_high" and (after_this, this)[k]:
                                    s_high(q * 2 + 2 - k, k)
                                if what == "y" and last:
                                    y_scaled(q * 2 - 2 + k, k, 2 * other + k)
                                if what == "y_high" and last:
                                    y_high(q * 2 - 2 + k, k)
                    skewed(act, pair)

                @block.tensor
                def _(pe):
                    def logits_of(t):
                        after(pe, exp_ready, t)
                        for c in range(NC):
                            span = slice(c * CH, (c + 1) * CH)
                            nc.tensor.matmul(logits[:, span], query[:, cols(t)], key_hi[:, span], start=True, stop=False)
                            done = nc.tensor.matmul(logits[:, span], query[:, cols(t)], key_lo[:, span],
                                                    start=False, stop=True)
                        done.then_inc(logits_done, 1)

                    for k in range(2):
                        logits_of(k)

                    def s_sum(t, k, y_read):
                        pe.wait_ge(s_lo_ready, t + 1)
                        after(pe, y_ready, y_read)
                        after(pe, s_rcp_ready, t)
                        for j in range(NT):
                            nc.tensor.matmul(acc_a[:, 0:1], s_hi[:, k, j * P:(j + 1) * P], ones_h[:, :],
                                             start=(j == 0), stop=False)
                            done = nc.tensor.matmul(acc_a[:, 0:1], s_lo[:, k, j * P:(j + 1) * P], ones_h[:, :],
                                                    start=False, stop=(j == NT - 1))
                        done.then_inc(s_sum_done, 1)

                    def r_product(t, k):
                        pe.wait_ge(s_lo_ready, t + 1)
                        parts = [part[:, k, :].rearrange("p (j n) -> p j n", j=NT) for part in (s_hi, s_lo)]
                        after(pe, r_read, t)
                        nc.tensor.matmul(acc_r[:, :], ident_h[:, :], plane(vec_hi, t), start=True, stop=False)
                        nc.tensor.matmul(acc_r[:, :], ident_h[:, :], plane(vec_lo, t), start=False, stop=False)
                        product3(acc_r[:, :], lambda part, j: parts[part][:, j, :],
                                 lambda part, j: (vec_hi, vec_lo)[part][:, j, :], NT,
                                 opens=False).then_inc(r_done, 1)

                    def turn_a(u, k, chunks):
                        pe.wait_ge(kept_ready, u + 1)
                        for c in chunks:
                            if c >= 2:
                                pe.wait_ge(at_lo_ready, u * BLK + c - 1)
                            elif k == 1 or final:
                                after(pe, at_lo_ready, u * BLK - 1 + c)
                            elif c == 0:
                                after(pe, y_lo_ready, u)
                            for b in range(BLK):
                                j = c * BLK + b
                                done = nc.tensor.transpose(turn[:, c % 2, b * P:(b + 1) * P],
                                                           kept[:, k, j * P:(j + 1) * P], ident[:, :])
                            done.then_inc(a_turned, 1)

                    def a_product(u, row_sums):
                        pe.wait_ge(at_lo_ready, (u + 1) * BLK)
                        after(pe, y_ready, u)
                        if row_sums is not None:
                            pe.wait_ge(s_rcp_ready, row_sums)
                        product3(acc_a[:, :], lambda part, j: (at_hi, at_lo)[part][:, j, :],
                                 lambda part, j: (mov_hi, mov_lo)[part][:, j, :], NT).then_inc(a_done, 1)

                    def turn_y(u, k):
                        if k == 0:
                            pe.wait_ge(at_lo_ready, (u + 1) * BLK + 3)
                        pe.wait_ge(y_ready, u + 1)
                        for d in range(DT):
                            done = nc.tensor.transpose(turn[:, k, d * P:(d + 1) * P],
                                                       y_row[:, k, d * P:(d + 1) * P], ident[:, :])
                        done.then_inc(y_turned, 1)

                    def pair(q, half, before_last, last, this, after_this):
                        t, u = q * 2, q * 2 - 2
                        first_sum, second_sum = (t + 1, t + 2) if this and not final else (None, None)
                        if after_this:
                            logits_of(t + 2)
                        if last:
                            turn_a(u, 0, (0, 1))
                        if this and not final:
                            s_sum(t, 0, u if last else 0)
                        if last:
                            turn_a(u, 0, (2, 3))
                            if not final:
                                r_product(t - 1, 1)
                            a_product(u, first_sum)
                            turn_a(u + 1, 1, (0, 1))
                        if after_this:
                            logits_of(t + 3)
                        if last:
                            turn_a(u + 1, 1, (2, 3))
                        if this and not final:
                            s_sum(t + 1, 1, u + 1 if last else 0)
                        if this:
                            r_product(t, 0)
                        if last:
                            if not final:
                                turn_y(u, 0)
                            a_product(u + 1, second_sum)
                            if not final:
                                turn_y(u + 1, 1)
                        if this and final:
                            r_product(t + 1, 1)
                    skewed(pe, pair)

                @block.vector
                def _(dve):
                    ch = Chain(dve, search_step)

                    def maximum(t, slot):
                        dve.wait_ge(logits_done, t + 1)
                        ch.step(nc.vector.reduce_max(row_max[:, slot:slot + 1], logits[:, :], AX))
                        ch.join()
                        nc.vector.tensor_scalar(neg_max[:, slot:slot + 1], row_max[:, slot:slot + 1],
                                                -1.0 / (SQ * SQ), None, ALU.mult).then_inc(max_ready, 1)

                    def a_low(t, chunks):
                        for c in chunks:
                            dve.wait_ge(at_hi_ready, t * BLK + c + 1)
                            split_lo(at_lo[:, c * BLK:(c + 1) * BLK, :],
                                     turn[:, c % 2, :].rearrange("p (b n) -> p b n", b=BLK),
                                     at_hi[:, c * BLK:(c + 1) * BLK, :], SE).then_inc(at_lo_ready, 1)

                    def s_sum(t):
                        rcp = s_rcp[:, bass.ds(t, 1)]
                        dve.wait_ge(s_sum_done, t + 1)
                        ch.step(nc.vector.tensor_scalar(rcp, acc_a[:, 0:1], 1.0, 1e-12, ALU.add, ALU.max))
                        ch.join()
                        ch.step(nc.vector.reciprocal(rcp, rcp))
                        ch.join()
                        ch.step(nc.vector.tensor_scalar(rcp, rcp, 1.0 / SX, None, ALU.mult))
                        ch.join()
                        dve.sem_inc(s_rcp_ready, 1)

                    def r_out(q, k):
                        t = q * 2 + k
                        dve.wait_ge(r_done, t + 1)
                        dve.wait_ge(base_loaded[k], (q + 1) * 16)
                        dst = plane(r_rows[k], q) if final else row_in[:, k, :]
                        nc.vector.scalar_tensor_tensor(out=dst, in0=acc_r[:, :], scalar=s_rcp[:, bass.ds(t, 1)],
                                                       in1=row_in[:, k, :],
                                                       op0=ALU.mult, op1=ALU.add).then_inc(r_read, 1)

                    def y_low(t, k):
                        dve.wait_ge(y_hi_ready, t + 1)
                        split_lo(feat_lo[:, :, cols(t)], turn[:, k, :].rearrange("p (d n) -> p d n", d=DT),
                                 feat_hi[:, :, cols(t)], SX).then_inc(y_lo_ready, 1)

                    def y_sum(q, k, slot):
                        t = q * 2 - 2 + k
                        dve.wait_ge(a_done, t + 1)
                        dve.wait_ge(r_read, t + 1)
                        after(dve, out_stored[k], (q - 1) * 16)
                        nc.vector.scalar_tensor_tensor(out=y_row[:, k, :], in0=acc_a[:, :],
                                                       scalar=a_rcp[:, slot:slot + 1], in1=plane(r_rows[k], q - 1),
                                                       op0=ALU.mult, op1=ALU.add).then_inc(y_ready, 1)
                        dve.wait_ge(y_ready, t + 1)
                        ch.step(nc.vector.bn_stats(stats[:, k, :], y_row[:, k, :]))
                        ch.join()
                        ch.step(nc.vector.bn_aggr(mean_var[:, k, :], stats[:, k, :]))
                        ch.join()
                        nc.vector.tensor_scalar(mean_var[:, k, 1:2], mean_var[:, k, 1:2], LN_EPS, None,
                                                ALU.add).then_inc(var_ready, 1)

                    def normalise(q, k):
                        dve.wait_ge(rstd_ready, q * 2 - 3 + k)
                        nc.vector.tensor_scalar(y_row[:, k, :], y_row[:, k, :], mean_var[:, k, 0:1], rstd[:, k:k + 1],
                                                ALU.subtract, ALU.mult).then_inc(normed, 1)

                    def halve(slot, h):
                        gain, miss = steps[h]
                        ch.step(nc.vector.scalar_tensor_tensor(
                            out=scrap[:, 0, :], in0=e[:, slot, :], scalar=thr[:, slot:slot + 1], in1=e[:, slot, :],
                            op0=ALU.is_gt, op1=ALU.mult, accum_out=above[:, 0:1]))
                        ch.join()
                        ch.step(nc.vector.tensor_scalar(hit[:, 0:1], above[:, 0:1], goal[:, slot:slot + 1], gain,
                                                        ALU.is_ge, ALU.mult))
                        ch.join()
                        ch.step(nc.vector.tensor_scalar(thr[:, slot:slot + 1], hit[:, 0:1], miss, thr[:, slot:slot + 1],
                                                        ALU.add, ALU.mult))
                        ch.join()

                    def locate(half, tiles):
                        for k in tiles:
                            slot = 2 * half + k
                            ch.step(nc.vector.scalar_tensor_tensor(
                                out=kept[:, k, :], in0=e[:, slot, :], scalar=thr[:, slot:slot + 1], in1=e[:, slot, :],
                                op0=ALU.is_lt, op1=ALU.mult, accum_out=under[:, k:k + 1]))
                            ch.join()
                            ch.step(nc.vector.max(top8[:, k, :], kept[:, k, :]))
                            ch.step(nc.vector.tensor_tensor(above[:, k:k + 1], total[:, slot:slot + 1],
                                                            under[:, k:k + 1], ALU.subtract))
                            ch.join()
                            ch.step(nc.vector.tensor_tensor_scan(cum8[:, k, :], ones8[:, :], top8[:, k, :],
                                                                 above[:, k:k + 1], ALU.mult, ALU.add))
                            ch.join()
                            ch.step(nc.vector.scalar_tensor_tensor(
                                out=reached8[:, k, 0:7], in0=cum8[:, k, 0:7], scalar=goal[:, slot:slot + 1],
                                in1=top8[:, k, 0:7], op0=ALU.is_ge, op1=ALU.mult))
                            ch.step(nc.vector.tensor_copy(reached8[:, k, 7:8], top8[:, k, 7:8]))
                            ch.join()
                            ch.step(nc.vector.reduce_max(edge[:, k:k + 1], reached8[:, k, :], AX))
                            ch.join()
                            ch.step(nc.vector.scalar_tensor_tensor(
                                out=kept[:, k, :], in0=e[:, slot, :], scalar=edge[:, k:k + 1], in1=e[:, slot, :],
                                op0=ALU.is_ge, op1=ALU.mult, accum_out=sum_ge[:, k:k + 1]))
                            ch.step(nc.vector.scalar_tensor_tensor(
                                out=cum8[:, k, :], in0=top8[:, k, :], scalar=edge[:, k:k + 1], in1=top8[:, k, :],
                                op0=ALU.is_gt, op1=ALU.mult, accum_out=sum_gt[:, k:k + 1]))

                    def weigh(half):
                        goals = goal[:, 2 * half:2 * half + 2]
                        ch.step(nc.vector.tensor_tensor(sum_gt[:, :], sum_gt[:, :], above[:, :], ALU.add))
                        ch.step(nc.vector.reciprocal(rcp_edge[:, :], edge[:, :]))
                        ch.step(nc.vector.scalar_tensor_tensor(out=hold[:, :], in0=goals, scalar=1.0 - SLACK,
                                                               in1=sum_ge[:, :], op0=ALU.mult, op1=ALU.is_gt))
                        ch.join()
                        ch.step(nc.vector.tensor_tensor(n_tied[:, :], sum_ge[:, :], sum_gt[:, :], ALU.subtract))
                        ch.step(nc.vector.tensor_tensor(n_kept[:, :], goals, sum_gt[:, :], ALU.subtract))
                        ch.join()
                        ch.step(nc.vector.tensor_tensor(n_tied[:, :], n_tied[:, :], rcp_edge[:, :], ALU.mult))
                        ch.step(nc.vector.tensor_tensor(n_kept[:, :], n_kept[:, :], rcp_edge[:, :], ALU.mult))
                        ch.join()
                        ch.step(nc.vector.tensor_scalar(n_tied[:, :], n_tied[:, :], ROUND, ROUND, ALU.add, ALU.subtract))
                        ch.step(nc.vector.tensor_scalar(n_kept[:, :], n_kept[:, :], 0.495, ROUND, ALU.add, ALU.add))
                        ch.join()
                        ch.step(nc.vector.tensor_scalar(n_tied[:, :], n_tied[:, :], 1.0, None, ALU.max))
                        ch.step(nc.vector.tensor_scalar(n_kept[:, :], n_kept[:, :], ROUND, 1.0, ALU.subtract, ALU.max))
                        ch.join()
                        ch.step(nc.vector.tensor_tensor(n_kept[:, :], n_kept[:, :], n_tied[:, :], ALU.min))
                        ch.step(nc.vector.reciprocal(rcp_tied[:, :], n_tied[:, :]))
                        ch.join()
                        ch.step(nc.vector.tensor_tensor(cut[:, :], n_tied[:, :], n_kept[:, :], ALU.subtract))
                        ch.join()
                        ch.step(nc.vector.tensor_scalar(n_kept[:, :], cut[:, :], 1.0, None, ALU.min))
                        ch.step(nc.vector.tensor_tensor(cut[:, :], cut[:, :], edge[:, :], ALU.mult))
                        ch.join()
                        ch.step(nc.vector.scalar_tensor_tensor(out=n_kept[:, :], in0=hold[:, :], scalar=16.0,
                                                               in1=n_kept[:, :], op0=ALU.mult, op1=ALU.max))
                        ch.step(nc.vector.tensor_tensor(kept_sum[:, :], sum_ge[:, :], cut[:, :], ALU.subtract))
                        ch.join()
                        ch.step(nc.vector.reduce_max(code32[:, 0:1], n_kept[:, :], AX))
                        ch.step(nc.vector.tensor_tensor(cut[:, :], cut[:, :], rcp_tied[:, :], ALU.mult))
                        ch.step(nc.vector.reciprocal(kept_sum[:, :], kept_sum[:, :]))
                        ch.join()
                        ch.step(nc.vector.transpose(code_t[:, :], code32[:, :]))
                        ch.step(nc.vector.tensor_scalar(a_rcp[:, 2 * half:2 * half + 2], kept_sum[:, :],
                                                        1.0 / (SE * SX), None, ALU.mult))
                        ch.join()
                        ch.step(nc.vector.reduce_max(code_4[:, 0:1], code_t[:, :], AX))
                        ch.join()
                        for r in range(1, 4):
                            ch.step(nc.vector.tensor_copy(code_4[0:1, r:r + 1], code_4[r * 32:r * 32 + 1, 0:1]))
                        ch.join()
                        ch.step(nc.vector.reduce_max(code_i[0:1, :], code_4[0:1, :], AX))
                        ch.restart()

                    def code():
                        return dve.value_load(code_i[0:1, 0:1], min_val=0, max_val=16)

                    def keep(q, half):
                        after(dve, y_ready, q * 2 - 2)
                        weigh(half)
                        with dve.While(lambda: code() >= 16):
                            for k in range(2):
                                slot_thr = thr[:, 2 * half + k:2 * half + k + 1]
                                ch.step(nc.vector.tensor_scalar(hit[:, k:k + 1], hold[:, k:k + 1], -1.0, 1.0,
                                                                ALU.mult, ALU.add))
                                ch.join()
                                ch.step(nc.vector.tensor_tensor(hit[:, k:k + 1], hit[:, k:k + 1], slot_thr,
                                                                ALU.mult))
                                ch.join()
                                ch.step(nc.vector.tensor_tensor(slot_thr, hit[:, k:k + 1], edge[:, k:k + 1],
                                                                ALU.max))
                                ch.join()
                            locate(half, (0, 1))
                            ch.join()
                            weigh(half)
                        with dve.If(code() >= 1):
                            for k in range(2):
                                slot = 2 * half + k
                                ch.step(nc.vector.tensor_scalar(e[:, slot, :], kept[:, k, :], edge[:, k:k + 1],
                                                                cut[:, k:k + 1], ALU.is_equal, ALU.mult))
                                ch.join()
                                ch.step(nc.vector.tensor_tensor(kept[:, k, :], kept[:, k, :], e[:, slot, :],
                                                                ALU.subtract))
                                ch.join()
                            ch.restart()
                        dve.sem_inc(kept_ready, 2)

                    for k in range(2):
                        maximum(k, k)
                    ch.restart()

                    def pair(q, half, before_last, last, this, after_this):
                        other = 1 - half
                        if this:
                            dve.wait_ge(thr_final[0], q + 1)
                        for h in range(halvings + 2):
                            if this:
                                if by_act[0] <= h < halvings:
                                    halve(2 * half, h)
                                if h == halvings:
                                    locate(half, (0,))
                                if h > halvings:
                                    dve.wait_ge(thr_final[1], q + 1)
                                    locate(half, (1,))
                                    ch.join()
                                    keep(q, half)
                            for what, k, *chunks in DVE_AFTER[p].get(h, ()):
                                if what == "a_low" and last:
                                    a_low(q * 2 - 2 + k, *chunks)
                                if what == "max" and after_this:
                                    maximum(q * 2 + 2 + k, 2 * other + k)
                                if what == "s_sum" and this:
                                    s_sum(q * 2 + k)
                                if what == "r_out" and this:
                                    r_out(q, k)
                                if what == "r_out_last" and last:
                                    r_out(q - 1, k)
                                if what == "y_low" and last:
                                    y_low(q * 2 - 2 + k, k)
                                if what == "y_sum" and last:
                                    y_sum(q, k, 2 * other + k)
                                if what == "normalise" and before_last:
                                    normalise(q, k)
                        ch.restart()
                    skewed(dve, pair)

        stage_norm()
        for p in range(2):
            stage_project(p)
            stage_multiply(p)


def kernel(x, adj, L0_gnn_W1, L0_gnn_W2, L0_gnn_W3, L0_gnn_U1_0, L0_gnn_U1_1, L0_gnn_U2_0, L0_gnn_U2_1,
           L0_gnn_gamma, L0_gnn_beta):
    import numpy as np
    import concourse.bacc as bacc
    from concourse.bass_utils import run_bass_kernel_spmd

    n = x.shape[0]
    adj_t = np.ascontiguousarray(np.asarray(adj).reshape(n // P, P, n // P, P).transpose(0, 3, 2, 1))
    given = {
        "x": x, "adj_t": adj_t.reshape(n // P, P, n), "w1_t": np.asarray(L0_gnn_W1).T, "w2": L0_gnn_W2,
        "w3": L0_gnn_W3, "u1_0": L0_gnn_U1_0, "u1_1": L0_gnn_U1_1, "u2_0": L0_gnn_U2_0, "u2_1": L0_gnn_U2_1,
        "gamma": L0_gnn_gamma, "beta": L0_gnn_beta,
    }
    nc = bacc.Bacc("TRN2", target_bir_lowering=False, num_devices=1)
    arrays, args = {}, []
    for name, a in given.items():
        arrays[name] = np.ascontiguousarray(a)
        args.append(nc.dram_tensor(name, arrays[name].shape, mybir.dt.from_np(arrays[name].dtype),
                                   kind="ExternalInput").ap())
    args.append(nc.dram_tensor("out", x.shape, F32, kind="ExternalOutput").ap())
    gnn_layer(nc, *args)
    return run_bass_kernel_spmd(nc, [arrays], core_ids=[0]).results[0]["out"]
```
